# Optimizing a Trainium2 kernel written in Bass

```python
import numpy as np
import jax
import jax.numpy as jnp

def _softmax(x, axis=-1):
    return jax.nn.softmax(x, axis=axis)

def _gelu(x):
    return jax.nn.gelu(x, approximate=True)

def _silu(x):
    return jax.nn.silu(x)

def _sigmoid(x):
    return jax.nn.sigmoid(x)

def _layernorm(x, axis=-1, eps=1e-05):
    m = jnp.mean(x, axis=axis, keepdims=True)
    v = jnp.var(x, axis=axis, keepdims=True)
    return (x - m) / jnp.sqrt(v + eps)

def _scatter_add(tgt, idx, src, axis=0):
    return tgt.at[idx].add(src)

def _segment_sum(src, seg, n):
    return jax.ops.segment_sum(src, seg, n)
kernel_name = 'mk_decoder_preln_d1_seqx_r2_f0b5b6'

def setup_inputs(seed: int=0):
    np.random.seed(seed)
    _w = jnp.asarray

    def _rec_inputs():
        import jax
        import jax.numpy as jnp
        _rk = jax.random.key(seed)
        x = 7.22e-05 + 1 * jax.random.normal(jax.random.fold_in(_rk, 1), (2, 2048, 512), jnp.float32)
        _lenS = 2048 - jax.random.randint(jax.random.fold_in(_rk, 7), (2,), 0, max(1, 2048 // 4) + 1, jnp.int32)
        _lenS2 = 77 - jax.random.randint(jax.random.fold_in(_rk, 8), (2,), 0, max(1, 77 // 4) + 1, jnp.int32)
        _ctx_1024P = jax.random.normal(jax.random.fold_in(_rk, 11), (2, 16, 512), jnp.float32)
        _ctx_1024c = jax.random.dirichlet(jax.random.fold_in(_rk, 511), 0.3 * jnp.ones((16,), jnp.float32), (2, 77))
        _ctx_1024t = jnp.einsum('bsk,bkd->bsd', _ctx_1024c, _ctx_1024P)
        _ctx_1024t = _ctx_1024t * jax.lax.rsqrt(jnp.mean(jnp.square(_ctx_1024t)) + 1e-12) * 0.953939
        ctx_1024 = -4.77421e-07 + 0.031248 * (_ctx_1024t + 0.3 * jax.random.normal(jax.random.fold_in(_rk, 611), (2, 77, 512), jnp.float32))
        return (x, ctx_1024)
    x, ctx_1024 = _rec_inputs()

    def _L0_attn_setup():
        import jax, jax.numpy as jnp
        import numpy as np
        B, S, D, H = (4, 1024, 512, 16)
        DK = D // H

        def apply_rope(x, pos, inv_freq):
            sincos = pos[:, :, None].astype(jnp.float32) * inv_freq
            sin = jnp.repeat(jnp.sin(sincos), 2, axis=-1)[:, None]
            cos = jnp.repeat(jnp.cos(sincos), 2, axis=-1)[:, None]
            x_rot = jnp.stack([-x[..., 1::2], x[..., ::2]], axis=-1).reshape(x.shape)
            return x * cos + x_rot * sin
        key = jax.random.key(seed)
        ks = jax.random.split(key, 5)
        scale = 1.0 / np.sqrt(D)
        x = jax.random.normal(ks[0], (B, S, D), dtype=jnp.float32)
        W_q = jax.random.normal(ks[1], (D, D), dtype=jnp.float32) * scale
        W_k = jax.random.normal(ks[2], (D, D), dtype=jnp.float32) * scale
        W_v = jax.random.normal(ks[3], (D, D), dtype=jnp.float32) * scale
        W_o = jax.random.normal(ks[4], (D, D), dtype=jnp.float32) * scale
        return {'x': x, 'W_q': W_q, 'W_k': W_k, 'W_v': W_v, 'W_o': W_o}
    _L0_attn_all = _L0_attn_setup()
    _L0_attn_in = {k: v for k, v in _L0_attn_all.items() if k in ('W_q', 'W_k', 'W_v', 'W_o')}
    del _L0_attn_all

    def _L0_xattn_setup():
        import jax, jax.numpy as jnp
        import numpy as np
        E, T, H, F = (8, 512, 512, 2048)
        key = jax.random.key(seed)
        k1, k2, k3 = jax.random.split(key, 3)
        x = jax.random.normal(k1, (E, T, H), dtype=jnp.float32)
        w1 = jax.random.normal(k2, (E, F, H), dtype=jnp.float32) * (1.0 / np.sqrt(H))
        w2 = jax.random.normal(k3, (E, F, H), dtype=jnp.float32) * (1.0 / np.sqrt(F))
        return {'x': x, 'w1': w1, 'w2': w2}
    _L0_xattn_all = _L0_xattn_setup()
    _L0_xattn_in = {k: v for k, v in _L0_xattn_all.items() if k in ()}
    del _L0_xattn_all

    def _L0_ffn_setup():
        import jax, jax.numpy as jnp
        import numpy as np
        MAX_VAL = 100.0
        key = jax.random.key(seed)
        k1, k2, k3 = jax.random.split(key, 3)
        B, S, D_IN, D_OUT = (4, 4096, 512, 512)
        x = jax.random.normal(k1, (B, S, D_IN), dtype=jnp.float32)
        weights = jax.random.normal(k2, (D_OUT, D_IN), dtype=jnp.float32)
        scale = jnp.ones((D_OUT,), dtype=jnp.float32)
        bias = jax.random.normal(k3, (D_OUT,), dtype=jnp.float32)
        return {'x': x, 'weights': weights, 'scale': scale, 'bias': bias}
    _L0_ffn_all = _L0_ffn_setup()
    _L0_ffn_in = {k: v for k, v in _L0_ffn_all.items() if k in ('weights', 'scale', 'bias')}
    del _L0_ffn_all
    return {'x': x, 'ctx_1024': ctx_1024, 'L0_attn_W_q': _L0_attn_in['W_q'], 'L0_attn_W_k': _L0_attn_in['W_k'], 'L0_attn_W_v': _L0_attn_in['W_v'], 'L0_attn_W_o': _L0_attn_in['W_o'], 'L0_ffn_weights': _L0_ffn_in['weights'], 'L0_ffn_scale': _L0_ffn_in['scale'], 'L0_ffn_bias': _L0_ffn_in['bias']}

def reference(x, ctx_1024, L0_attn_W_q, L0_attn_W_k, L0_attn_W_v, L0_attn_W_o, L0_ffn_weights, L0_ffn_scale, L0_ffn_bias):
    import jax
    import jax.numpy as jnp

    def _L0_attn_ref(x, W_q, W_k, W_v, W_o):
        import jax, jax.numpy as jnp
        import numpy as np
        B, S, D, H = (4, 1024, 512, 16)
        DK = D // H

        def apply_rope(x, pos, inv_freq):
            sincos = pos[:, :, None].astype(jnp.float32) * inv_freq
            sin = jnp.repeat(jnp.sin(sincos), 2, axis=-1)[:, None]
            cos = jnp.repeat(jnp.cos(sincos), 2, axis=-1)[:, None]
            x_rot = jnp.stack([-x[..., 1::2], x[..., ::2]], axis=-1).reshape(x.shape)
            return x * cos + x_rot * sin
        b, s, _ = x.shape
        pos = jnp.arange(s)[None, :]
        inv_freq = 1.0 / 10000.0 ** (jnp.arange(0, DK, 2, dtype=jnp.float32) / DK)

        def proj(W):
            return (x @ W.T).reshape(b, s, H, DK).transpose(0, 2, 1, 3)
        Q = apply_rope(proj(W_q), pos, inv_freq)
        K = apply_rope(proj(W_k), pos, inv_freq)
        V = proj(W_v)
        scores = jnp.einsum('bhqd,bhkd->bhqk', Q, K) / jnp.sqrt(jnp.float32(DK))
        attn = jax.nn.softmax(scores, axis=-1)
        out = jnp.einsum('bhqk,bhkd->bhqd', attn, V)
        out = out.transpose(0, 2, 1, 3).reshape(b, s, D)
        return out @ W_o.T

    def _L0_xattn_ref(x, w1, w2):
        import jax, jax.numpy as jnp
        import numpy as np
        E, T, H, F = (8, 512, 512, 2048)
        h = jnp.einsum('eth,efh->etf', x, w1)
        g = jax.nn.gelu(h, approximate=True)
        out = jnp.einsum('etf,efh->eth', g, w2)
        return out

    def _L0_ffn_ref(x, weights, scale, bias):
        import jax, jax.numpy as jnp
        import numpy as np
        MAX_VAL = 100.0
        w = (weights >= 0.0).astype(x.dtype) * 2.0 - 1.0
        y = jnp.einsum('bsi,oi->bso', x, w)
        y = y * scale + bias
        y = jnp.clip(y, -MAX_VAL, MAX_VAL)
        return y
    x = x + _L0_attn_ref(_layernorm(x, axis=-1), L0_attn_W_q, L0_attn_W_k, L0_attn_W_v, L0_attn_W_o)
    x = x + _L0_xattn_ref(_layernorm(x, axis=-1), ctx_1024, ctx_1024)
    x = x + _L0_ffn_ref(_layernorm(x, axis=-1), L0_ffn_weights, L0_ffn_scale, L0_ffn_bias)
    return x

_drawn_inputs = setup_inputs


def setup_inputs(seed=0):
    import zlib

    import numpy as np

    out = dict(_drawn_inputs(seed))
    spreads = {'L0_ffn_scale': (1.0, 0.2)}
    factors = {}
    for name, (base, spread) in spreads.items():
        noise = np.random.default_rng([zlib.crc32(name.encode()), seed]).standard_normal(out[name].shape)
        drawn = base * np.exp(spread * noise) if base else spread * noise
        out[name] = jnp.asarray(drawn.astype(out[name].dtype))
    for name, factor in factors.items():
        out[name] = (out[name] * factor).astype(out[name].dtype)
    return out
```

```python
from contextlib import ExitStack

import numpy as np

import concourse.bass as bass
from concourse import mybir

F32 = mybir.dt.float32
F16 = mybir.dt.float16
ALU = mybir.AluOpType
ACT = mybir.ActivationFunctionType
AX_X = mybir.AxisListType.X

P = 128
B, S, D = 2, 2048, 512
H = 16
DK = D // H
T = 77
NTOK = B * S
CH = D // P
BLK = 512
TB = BLK // P
NBLK = NTOK // BLK
WS = 64.0
EPS = 1e-5
CLIP = 100.0
SM_SCALE = 1.0 / float(np.sqrt(np.float32(DK)))

KT = S // P
UQ = 1024
NU = B * H * S // UQ
NSTEP = NU * KT
SR = 3 * DK
MR = SR
AHEAD = 22
NP = 4


def after(eng, sem, count):
    if isinstance(count, int) and count <= 0:
        return
    eng.wait_ge(sem, count)


def apart(eng, passed, *waits):
    for sem, c in waits:
        after(eng, sem, c)
    eng.sem_inc(passed)


def decoder_layer(nc, x, ctx_in, wq, wk, wv, wo, wf, fscale, fbias, ident_in, rot_in, cos_in, sin_in, out):
    q_scr = nc.dram_tensor("q_scr", (B, 2, D, S), F16, kind="Internal").ap()
    k_scr = nc.dram_tensor("k_scr", (B, 2, D, S), F16, kind="Internal").ap()
    att_scr = nc.dram_tensor("att_scr", (B, S, D), F32, kind="Internal").ap()
    x_t = x.rearrange("b (n t p) d -> b n p t d", t=TB, p=P)
    out_t = out.rearrange("b (n t p) d -> b n p t d", t=TB, p=P)
    att_t = att_scr.rearrange("b (n t p) d -> b n p t d", t=TB, p=P)

    with ExitStack() as top:
        def sb(name, shape, dt, st=top):
            return st.enter_context(nc.sbuf_tensor(name, shape, dt))

        def sem(name, st=top):
            return st.enter_context(nc.semaphore(name))

        ps = top.enter_context(nc.psum_tensor("ps", [P, 8, 512], F32))
        wT = {m: sb(f"{m}T", [P, 2, CH, D], F16) for m in ("wq", "wk", "wv", "wo")}
        wfT = sb("wfT", [P, CH, D], F16)
        ctxT = sb("ctxT", [P, B, 2, CH, T], F16)
        ctxr = sb("ctxr", [T, B, 2, D], F16)
        ident = sb("ident", [P, P], F32)
        fsc = sb("fsc", [P, D], F32)
        fbi = sb("fbi", [P, D], F32)

        weights(nc, sb, sem, ps, wT, wfT, ctxT, ctxr, ident, fsc, fbi,
                ctx_in, wq, wk, wv, wo, wf, fscale, fbias, ident_in)
        with ExitStack() as mid:
            v_all = sb("v_all", [P, B * KT, D], F32, mid)
            project(nc, sb, sem, ps, wT, ident, v_all, x_t, rot_in, cos_in, sin_in, q_scr, k_scr)
            attend(nc, sb, sem, ps, ident, v_all, q_scr, k_scr, att_scr)
        tail(nc, sb, sem, ps, wT, wfT, ctxT, ctxr, ident, fsc, fbi, x_t, att_t, out_t)


def weights(nc, sb, sem, ps, wT, wfT, ctxT, ctxr, ident, fsc, fbi,
            ctx_in, wq, wk, wv, wo, wf, fscale, fbias, ident_in):
    with ExitStack() as st:
        wraw = sb("wraw", [P, 5, CH, D], F32, st)
        craw = sb("craw", [T, B, D], F32, st)
        w_in = [sem(f"w_in{i}", st) for i in range(5)]
        c_in = sem("c_in", st)
        sc_in = sem("sc_in", st)
        id_in = sem("id_in", st)
        signed = sem("signed", st)
        turned = sem("turned", st)
        hi_done = sem("hi_done", st)
        lo_done = sem("lo_done", st)
        c_hi = sem("c_hi", st)
        NB = 8
        jobs = [(m, c) for m in range(4) for c in range(CH)] + [(4, c) for c in range(CH)] + [(5, b) for b in range(B)]
        mats = ("wq", "wk", "wv", "wo")
        los = [sum(1 for m, _ in jobs[:j + 1] if m != 4) for j in range(len(jobs))]

        def dst(j, half):
            m, c = jobs[j]
            if m < 4:
                return wT[mats[m]][:, half, c, :]
            if m == 4:
                return wfT[:, c, :]
            return ctxT[:, c, half, :, :]

        def src(j):
            if jobs[j][0] == 5:
                return ps[:, j % NB, :].rearrange("p (c t) -> p c t", c=CH)[:, :, 0:T]
            return ps[:, j % NB, :]

        with nc.Block() as block:
            @block.sync
            def _(sp):
                sp.dma_start(ident[:, :], ident_in).then_inc(id_in, 16)
                for i, w in enumerate((wq, wk, wv, wo, wf)):
                    sp.dma_start(wraw[:, i, :, :], w.rearrange("(o p) i -> p o i", p=P)).then_inc(w_in[i], 16)
                sp.dma_start(craw[:, :, :], ctx_in.rearrange("b t d -> t b d")).then_inc(c_in, 16)
                sp.dma_start(fsc[:, :], fscale.rearrange("(a d) -> a d", a=1).broadcast_to([P, D])).then_inc(sc_in, 16)
                sp.dma_start(fbi[:, :], fbias.rearrange("(a d) -> a d", a=1).broadcast_to([P, D])).then_inc(sc_in, 16)
                sp.wait_ge(sc_in, 32)

            @block.tensor
            def _(pe):
                pe.wait_ge(id_in, 16)
                for j, (m, c) in enumerate(jobs):
                    if c == 0:
                        if m == 4:
                            pe.wait_ge(signed, 1)
                        elif m == 5:
                            pe.wait_ge(c_in, 16)
                        else:
                            pe.wait_ge(w_in[m], 16)
                    if j >= NB:
                        pe.wait_ge(hi_done, j - NB + 1)
                        pe.wait_ge(lo_done, los[j - NB])
                    for o in range(CH):
                        if m == 5:
                            ins = pe.transpose(ps[:, j % NB, o * P:o * P + T], craw[:, c, o * P:(o + 1) * P], ident[0:T, 0:T])
                        else:
                            ins = pe.transpose(ps[:, j % NB, o * P:(o + 1) * P], wraw[:, m, o, c * P:(c + 1) * P], ident[:, :])
                    ins.then_inc(turned, 1)

            @block.scalar
            def _(act):
                for j, (m, _) in enumerate(jobs):
                    act.wait_ge(turned, j + 1)
                    act.activation(dst(j, 0), src(j), ACT.Copy, scale=1.0 if m == 4 else WS).then_inc(hi_done, 1)
                for b in range(B):
                    act.activation(ctxr[:, b, 0, :], craw[:, b, :], ACT.Copy, scale=WS).then_inc(c_hi, 1)

            @block.vector
            def _(dve):
                dve.wait_ge(w_in[4], 16)
                dve.tensor_scalar(wraw[:, 4, :, :], wraw[:, 4, :, :], 0.0, 0.5, ALU.is_ge, ALU.subtract).then_inc(signed, 1)
                for j, (m, _) in enumerate(jobs):
                    if m != 4:
                        dve.wait_ge(hi_done, j + 1)
                        dve.scalar_tensor_tensor(dst(j, 1), src(j), WS, dst(j, 0), ALU.mult, ALU.subtract).then_inc(lo_done, 1)
                for b in range(B):
                    dve.wait_ge(c_hi, b + 1)
                    dve.scalar_tensor_tensor(ctxr[:, b, 1, :], craw[:, b, :], WS, ctxr[:, b, 0, :], ALU.mult, ALU.subtract)
                dve.wait_ge(sc_in, 32)
                dve.tensor_scalar(fsc[:, :], fsc[:, :], 2.0, None, ALU.mult)


def project(nc, sb, sem, ps, wT, ident, v_all, x_t, rot_in, cos_in, sin_in, q_scr, k_scr):
    NT = 2 * CH
    with ExitStack() as st:
        rot = sb("rot", [P, P], F32, st)
        cos = sb("cos", [P, S], F32, st)
        sin = sb("sin", [P, S], F32, st)
        xin = sb("xin", [P, 2, TB, D], F32, st)
        xh = sb("xh", [P, TB, D], F32, st)
        xT = sb("xT", [P, 2, 2, CH, BLK], F16, st)
        stat = sb("stat", [P, TB, 6], F32, st)
        mv = sb("mv", [P, TB, 2], F32, st)
        var = sb("var", [P, TB], F32, st)
        std = sb("std", [P, TB], F32, st)
        rstd = sb("rstd", [P, TB], F32, st)
        raw = sb("raw", [P, 2, BLK], F32, st)
        rs = sb("rs", [P, 2, BLK], F32, st)
        rc = sb("rc", [P, 2, BLK], F32, st)
        ro = sb("ro", [P, 2, BLK], F32, st)
        pair = sb("pair", [P, 2, 2, BLK], F16, st)
        tab_in = sem("tab_in", st)
        x_in = [sem(f"x_in{i}", st) for i in range(2)]
        stats = sem("stats", st)
        aggr = sem("aggr", st)
        var_ok = sem("var_ok", st)
        std_ok = sem("std_ok", st)
        rstd_ok = sem("rstd_ok", st)
        normed = sem("normed", st)
        turned = sem("turned1", st)
        xhi = sem("xhi", st)
        xlo = sem("xlo", st)
        proj = sem("proj", st)
        raw_ok = sem("raw_ok", st)
        rot_ok = sem("rot_ok", st)
        rs_ok = sem("rs_ok", st)
        rc_ok = sem("rc_ok", st)
        ro_ok = sem("ro_ok", st)
        phi = sem("phi", st)
        plo = sem("plo", st)
        stored = [sem(f"stored{i}", st) for i in range(2)]
        vps = sem("vps", st)
        v_ok = sem("v_ok", st)
        dve_passed = sem("dve_passed", st)
        pool_passed = sem("pool_passed", st)

        def loop(eng, body):
            for b in range(B):
                body(0, b)
            with eng.Fori(1, NBLK // 2) as i:
                for b in range(B):
                    body(i, b)

        with nc.Block() as block:
            @block.sync
            def _(sp):
                sp.dma_start(cos[:, :], cos_in).then_inc(tab_in, 16)
                sp.dma_start(sin[:, :], sin_in).then_inc(tab_in, 16)
                sp.dma_start(rot[:, :], rot_in).then_inc(tab_in, 16)
                for b in range(B):
                    sp.dma_start(xin[:, b, :, :], x_t[b, 0]).then_inc(x_in[b], 16)

                def body(i, b):
                    n = 2 * i + b
                    for o in range(NT):
                        g = NT * n + o
                        scr = q_scr if o < CH else k_scr
                        c = o % CH
                        for half, ok in ((0, phi), (1, plo)):
                            sp.wait_ge(ok, g + 1)
                            sp.dma_start(scr[b, half, c * P:(c + 1) * P, bass.ds(i * BLK, BLK)],
                                         pair[:, o % 2, half, :]).then_inc(stored[o % 2], 16)

                def load(i, b):
                    n = 2 * i + b
                    sp.wait_ge(normed, TB * (n - 1))
                    sp.dma_start(xin[:, b, :, :], x_t[b, i]).then_inc(x_in[b], 16)

                with sp.Fori(0, NBLK // 2 - 1) as i:
                    for b in range(B):
                        load(i + 1, b)
                        body(i, b)
                for b in range(B):
                    body(NBLK // 2 - 1, b)
                for o in range(2):
                    sp.wait_ge(stored[o], 16 * NT * NBLK)

            @block.vector
            def _(dve):
                dve.wait_ge(tab_in, 48)

                def norm(i, b):
                    n = 2 * i + b
                    dve.wait_ge(x_in[b], 16 * (i + 1))
                    for t in range(TB):
                        dve.bn_stats(stat[:, t, :], xin[:, b, t, :]).then_inc(stats, 1)
                    apart(dve, dve_passed, (stats, TB * (n + 1)))
                    for t in range(TB):
                        dve.bn_aggr(mv[:, t, :], stat[:, t, :]).then_inc(aggr, 1)
                    dve.wait_ge(aggr, TB * (n + 1))
                    dve.tensor_scalar(var[:, :], mv[:, :, 1], EPS, None, ALU.add).then_inc(var_ok, 1)
                    dve.wait_ge(std_ok, n + 1)
                    dve.reciprocal(rstd[:, :], std[:, :]).then_inc(rstd_ok, 1)
                    dve.wait_ge(rstd_ok, n + 1)
                    after(dve, turned, CH * n)
                    for t in range(TB):
                        dve.tensor_scalar(xh[:, t, :], xin[:, b, t, :], mv[:, t, 0:1], rstd[:, t:t + 1],
                                          ALU.subtract, ALU.mult).then_inc(normed, 1)

                def low(i, b):
                    n = 2 * i + b
                    for c in range(CH):
                        dve.wait_ge(xhi, CH * n + c + 1)
                        dve.tensor_tensor(xT[:, b, 1, c, :], ps[:, c % 2, :], xT[:, b, 0, c, :], ALU.subtract).then_inc(xlo, 1)

                def rope(i, b):
                    n = 2 * i + b
                    for o in range(NT + 1):
                        if o < NT:
                            g = NT * n + o
                            dve.wait_ge(rot_ok, g + 1)
                            after(dve, ro_ok, g - 1)
                            dve.tensor_tensor(rs[:, o % 2, :], ps[:, 4 + o % 2, :], sin[:, bass.ds(i * BLK, BLK)],
                                              ALU.mult).then_inc(rs_ok, 1)
                            dve.wait_ge(rs_ok, g + 1)
                            dve.wait_ge(rc_ok, g + 1)
                            after(dve, phi, g - 1)
                            after(dve, plo, g - 1)
                            dve.tensor_tensor(ro[:, o % 2, :], rs[:, o % 2, :], rc[:, o % 2, :], ALU.add).then_inc(ro_ok, 1)
                        if o >= 1:
                            g = NT * n + o - 1
                            dve.wait_ge(phi, g + 1)
                            dve.tensor_tensor(pair[:, (o - 1) % 2, 1, :], ro[:, (o - 1) % 2, :], pair[:, (o - 1) % 2, 0, :],
                                              ALU.subtract).then_inc(plo, 1)

                norm(0, 0)
                low(0, 0)
                norm(0, 1)
                low(0, 1)
                rope(0, 0)
                with dve.Fori(1, NBLK // 2) as i:
                    norm(i, 0)
                    low(i, 0)
                    rope(i - 1, 1)
                    norm(i, 1)
                    low(i, 1)
                    rope(i, 0)
                rope(NBLK // 2 - 1, 1)

            @block.tensor
            def _(pe):
                pe.wait_ge(tab_in, 48)

                def turn(i, b):
                    n = 2 * i + b
                    pe.wait_ge(normed, TB * (n + 1))
                    for c in range(CH):
                        g = CH * n + c
                        after(pe, xhi, g - 1)
                        after(pe, xlo, g - 1)
                        for t in range(TB):
                            ins = pe.transpose(ps[:, c % 2, t * P:(t + 1) * P], xh[:, t, c * P:(c + 1) * P], ident[:, :])
                        ins.then_inc(turned, 1)

                def three(dst, lhs, rhs):
                    k = 0
                    for c in range(CH):
                        for a, r in ((0, 0), (0, 1), (1, 0)):
                            ins = pe.matmul(dst, lhs(a, c), rhs(r, c), start=(k == 0), stop=(k == 3 * CH - 1))
                            k += 1
                    return ins

                def rotate(g, o):
                    pe.wait_ge(raw_ok, g + 1)
                    after(pe, rs_ok, g - 1)
                    pe.matmul(ps[:, 4 + o % 2, :], rot[:, :], raw[:, o % 2, :], start=True, stop=True).then_inc(rot_ok, 1)

                def multiply(i, b):
                    n = 2 * i + b
                    pe.wait_ge(xlo, CH * (n + 1))
                    for o in range(NT):
                        g = NT * n + o
                        w = wT["wq" if o < CH else "wk"]
                        c0 = (o % CH) * P
                        after(pe, raw_ok, g - 1)
                        three(ps[:, 2 + o % 2, :], lambda a, c: w[:, a, c, c0:c0 + P],
                              lambda r, c: xT[:, b, r, c, :]).then_inc(proj, 1)
                        if o >= 1:
                            rotate(g - 1, o - 1)
                    for t in range(TB):
                        g = TB * n + t
                        after(pe, v_ok, g - 1)
                        three(ps[:, 6 + t % 2, :], lambda a, c: xT[:, b, a, c, t * P:(t + 1) * P],
                              lambda r, c: wT["wv"][:, r, c, :]).then_inc(vps, 1)
                        if t == 0:
                            rotate(NT * (n + 1) - 1, NT - 1)

                turn(0, 0)
                turn(0, 1)
                multiply(0, 0)
                with pe.Fori(1, NBLK // 2) as i:
                    turn(i, 0)
                    multiply(i - 1, 1)
                    turn(i, 1)
                    multiply(i, 0)
                multiply(NBLK // 2 - 1, 1)

            @block.scalar
            def _(act):
                def high(i, b):
                    n = 2 * i + b
                    act.wait_ge(var_ok, n + 1)
                    act.activation(std[:, :], var[:, :], ACT.Sqrt).then_inc(std_ok, 1)
                    after(act, vps, TB * (n - 1))
                    for c in range(CH):
                        act.wait_ge(turned, CH * n + c + 1)
                        act.activation(xT[:, b, 0, c, :], ps[:, c % 2, :], ACT.Copy).then_inc(xhi, 1)

                def split(g, o):
                    act.wait_ge(ro_ok, g + 1)
                    if not (isinstance(g, int) and g < 2):
                        act.wait_ge(stored[o % 2], 16 * (g - o % 2))
                    act.activation(pair[:, o % 2, 0, :], ro[:, o % 2, :], ACT.Copy).then_inc(phi, 1)

                def evacuate(i, b):
                    n = 2 * i + b
                    for o in range(NT):
                        g = NT * n + o
                        act.wait_ge(proj, g + 1)
                        after(act, rot_ok, g - 1)
                        after(act, rc_ok, g - 1)
                        act.activation(raw[:, o % 2, :], ps[:, 2 + o % 2, :], ACT.Copy, scale=1.0 / WS).then_inc(raw_ok, 1)
                        if o >= 2:
                            split(g - 2, o - 2)
                    for t in range(TB):
                        act.wait_ge(vps, TB * n + t + 1)
                        act.activation(v_all[:, KT * b + i * TB + t, :],
                                       ps[:, 6 + t % 2, :], ACT.Copy, scale=1.0 / WS).then_inc(v_ok, 1)
                        if t < 2:
                            split(NT * (n + 1) - 2 + t, NT - 2 + t)

                high(0, 0)
                high(0, 1)
                evacuate(0, 0)
                with act.Fori(1, NBLK // 2) as i:
                    high(i, 0)
                    evacuate(i - 1, 1)
                    high(i, 1)
                    evacuate(i, 0)
                evacuate(NBLK // 2 - 1, 1)

            @block.gpsimd
            def _(pool):
                pool.wait_ge(tab_in, 48)

                def body(i, b):
                    n = 2 * i + b
                    for o in range(NT):
                        g = NT * n + o
                        apart(pool, pool_passed, (raw_ok, g + 1), (ro_ok, g - 1))
                        pool.tensor_tensor(rc[:, o % 2, :], raw[:, o % 2, :], cos[:, bass.ds(i * BLK, BLK)],
                                           ALU.mult).then_inc(rc_ok, 1)
                loop(pool, body)


def attend(nc, sb, sem, ps, ident, v_all, q_scr, k_scr, att_scr):
    UH = S // UQ
    QT = UQ // P
    KB = S // 512
    HS = UH * KT
    ITER = 2 * HS
    NHEAD = B * H
    with ExitStack() as st:
        qs = sb("qs", [MR + 1, 2, S], F16, st)
        ks = sb("ks", [MR + 1, 2, S], F16, st)
        vh = sb("vh", [P, 2, KT, 64], F32, st)
        pr = sb("pr", [P, NP, UQ], F32, st)
        rmax = sb("rmax", [P, QT, KB], F32, st)
        m8 = sb("m8", [P, QT], F32, st)
        mrow = sb("mrow", [QT, P], F16, st)
        ov = sb("ov", [P, 512], F32, st)
        rden = sb("rden", [P, QT], F32, st)
        att = sb("att", [P, 2, KT, DK], F32, st)
        qk_in = [sem(f"qk_in{i}", st) for i in range(2)]
        init = sem("init", st)
        v_copied = sem("v_copied", st)
        sc = sem("sc", st)
        ex = sem("ex", st)
        pv = sem("pv", st)
        mx = sem("mx", st)
        md = sem("md", st)
        m_all = sem("m_all", st)
        m_t = sem("m_t", st)
        m_r = sem("m_r", st)
        m_in = [sem(f"m_in{i}", st) for i in range(2)]
        ov_ok = sem("ov_ok", st)
        o_t = sem("o_t", st)
        den = sem("den", st)
        at_ok = sem("at_ok", st)
        at_out = [sem(f"at_out{i}", st) for i in range(2)]

        SC, MX, OV, MISC = 0, 4, 6, 7

        def head_of(s):
            return (s // HS) % 2

        def sweep(eng, step):
            for s in range(ITER):
                step(0, s)
            with eng.Fori(1, NHEAD // 2 - 1) as it:
                for s in range(ITER):
                    step(it, s)
            for s in range(ITER):
                step(NHEAD // 2 - 1, s)

        def exists(it, s):
            return not (isinstance(it, int) and ITER * it + s >= NSTEP)

        with nc.Block() as block:
            @block.gpsimd
            def _(pool):
                pool.memset(vh[:, :, :, DK:], 0.0).then_inc(init, 1)
                pool.wait_ge(init, 1)
                pool.memset(vh[:, :, :, DK:DK + 1], 1.0).then_inc(init, 1)
                pool.wait_ge(init, 2)
                pool.memset(ks[MR:MR + 1, :, :], 1.0).then_inc(init, 1)
                pool.wait_ge(init, 3)

                for b in range(B):
                    def body(i, b=b):
                        for par in range(2):
                            h = 2 * i + par + H * b
                            after(pool, pv, HS * (h - 1))
                            pool.tensor_copy(vh[:, par, :, 0:DK],
                                             v_all[:, b * KT:(b + 1) * KT, bass.ds((2 * i + par) * DK, DK)]).then_inc(v_copied, 1)
                    if b == 0:
                        body(0)
                    with pool.Fori(1 if b == 0 else 0, H // 2) as i:
                        body(i)

            @block.sync
            def _(sp):
                def load(b, i, par):
                    d0 = (2 * i + par) * DK
                    for r, half in enumerate((0, 1, 0)):
                        sp.dma_start(qs[r * DK:(r + 1) * DK, par, :], q_scr[b, half, bass.ds(d0, DK), :]).then_inc(qk_in[par], 16)
                    for r, half in enumerate((0, 0, 1)):
                        sp.dma_start(ks[r * DK:(r + 1) * DK, par, :], k_scr[b, half, bass.ds(d0, DK), :]).then_inc(qk_in[par], 16)

                def store_max(v):
                    it, w = v
                    u = 4 * it + w
                    par, uh = w // UH, w % UH
                    sp.wait_ge(m_r, u + 1)
                    sp.dma_start(qs[MR:MR + 1, par, uh * UQ:(uh + 1) * UQ], mrow[:, :]).then_inc(m_in[par], 16)

                def store_att(b, i, par):
                    h = 2 * i + par + H * b
                    sp.wait_ge(at_ok, UH * (h + 1))
                    sp.dma_start(att_scr[b].rearrange("(t p) d -> p t d", p=P)[:, :, bass.ds((2 * i + par) * DK, DK)],
                                 att[:, par, :, :]).then_inc(at_out[par], 16)

                load(0, 0, 0)
                load(0, 0, 1)
                store_max((0, 0))
                def heads(b, i, last):
                    base = H // 2 * b + i
                    nb, ni = (b + 1, 0) if isinstance(i, int) and i + 1 == H // 2 else (b, i + 1)
                    store_max((base, 1))
                    store_max((base, 2))
                    if not last:
                        sp.wait_ge(sc, ITER * base + HS)
                        load(nb, ni, 0)
                    store_att(b, i, 0)
                    store_max((base, 3))
                    if not last:
                        store_max((base + 1, 0))
                        sp.wait_ge(sc, ITER * base + 2 * HS)
                        load(nb, ni, 1)
                    store_att(b, i, 1)

                for b in range(B):
                    with sp.Fori(0, H // 2 - 1) as i:
                        heads(b, i, False)
                    heads(b, H // 2 - 1, b == B - 1)
                for par in range(2):
                    sp.wait_ge(at_out[par], 16 * NHEAD // 2)

            @block.tensor
            def _(pe):
                pe.wait_ge(init, 3)

                def maxima(it, s):
                    if not exists(it, s):
                        return
                    a = ITER * it + s
                    par, uh, k = head_of(s), (s // KT) % UH, s % KT
                    if s % HS == 0:
                        pe.wait_ge(qk_in[par], 96 * (it + 1 + (0 if s < ITER else 1)))
                    for j in range(2):
                        idx = 2 * k + j
                        qt, kb = idx // KB, idx % KB
                        after(pe, md, 2 * a + j - 1)
                        q0 = uh * UQ + qt * P
                        pe.matmul(ps[:, MX + j, :], qs[0:SR, par, q0:q0 + P], ks[0:SR, par, kb * 512:(kb + 1) * 512],
                                  start=True, stop=True).then_inc(mx, 1)

                def turn_max(it, s):
                    if s % KT != 1:
                        return
                    v = 4 * it + s // KT
                    if isinstance(v, int) and (v == 0 or v > NU):
                        return
                    pe.wait_ge(m_all, v)
                    after(pe, at_ok, v - 2)
                    pe.transpose(ps[0:QT, MISC, 0:P], m8[:, :], ident[:, :]).then_inc(m_t, 1)

                def scores(it, s):
                    g = ITER * it + s
                    par, uh, k = head_of(s), (s // KT) % UH, s % KT
                    if k == 0:
                        pe.wait_ge(m_in[par], 16 * (UH * it + uh + 1))
                    after(pe, ex, g - 1)
                    for j in range(2):
                        q0 = uh * UQ + j * 512
                        ins = pe.matmul(ps[:, SC + 2 * (s % 2) + j, :], ks[:, par, k * P:(k + 1) * P], qs[:, par, q0:q0 + 512],
                                        start=True, stop=True)
                    ins.then_inc(sc, 1)

                def values(it, s):
                    g = ITER * it + s
                    par, k = head_of(s), s % KT
                    if s % HS == 0:
                        pe.wait_ge(v_copied, 2 * it + par + 1)
                    if k == 0:
                        after(pe, ov_ok, 4 * it + s // KT)
                    pe.wait_ge(ex, g + 1)
                    for j in range(2):
                        ins = pe.matmul(ps[64 * j:64 * j + 64, OV, :], vh[:, par, k, :], pr[:, s % NP, j * 512:(j + 1) * 512],
                                        start=(k == 0), stop=(k == KT - 1), skip_group_check=True)
                    ins.then_inc(pv, 1)

                def turn_out(it, s):
                    if s % KT != 3:
                        return
                    u = 4 * it + s // KT
                    if isinstance(u, int) and u == 0:
                        return
                    pe.wait_ge(ov_ok, u)
                    pe.wait_ge(m_r, u + 1)
                    for c in range(4):
                        ins = pe.transpose(ps[:, MISC, c * P:(c + 1) * P], ov[:, c * P:(c + 1) * P], ident[:, :])
                    ins.then_inc(o_t, 1)

                def step(it, s):
                    scores(it, s)
                    sa = s + AHEAD
                    maxima(it, sa)
                    turn_max(it, sa)
                    if s >= 1:
                        values(it, s - 1)
                    elif not (isinstance(it, int) and it == 0):
                        values(it - 1, ITER - 1)
                    turn_out(it, s)

                for s in range(AHEAD):
                    maxima(0, s)
                    turn_max(0, s)
                sweep(pe, step)
                values(NHEAD // 2 - 1, ITER - 1)
                pe.wait_ge(ov_ok, NU)
                pe.wait_ge(at_ok, NU - 1)
                for c in range(4):
                    ins = pe.transpose(ps[:, MISC, c * P:(c + 1) * P], ov[:, c * P:(c + 1) * P], ident[:, :])
                ins.then_inc(o_t, 1)

            @block.scalar
            def _(act):
                def evacuate(u):
                    act.wait_ge(pv, KT * u)
                    after(act, o_t, u - 1)
                    act.activation(ov[:, :], ps[:, OV, :], ACT.Copy).then_inc(ov_ok, 1)

                def step(it, s):
                    g = ITER * it + s
                    act.wait_ge(sc, g + 1)
                    after(act, pv, g - NP + 1)
                    act.activation(pr[:, s % NP, :], ps[:, SC + 2 * (s % 2):SC + 2 * (s % 2) + 2, :].rearrange("p a n -> p (a n)"),
                                   ACT.Exp, scale=SM_SCALE).then_inc(ex, 1)
                    if s % KT == 0 and not (isinstance(it, int) and g == 0):
                        evacuate(4 * it + s // KT)

                sweep(act, step)
                evacuate(NU)

            @block.vector
            def _(dve):
                def maxima(it, s):
                    if not exists(it, s):
                        return
                    a = ITER * it + s
                    u = 4 * it + s // KT
                    if s % KT == 0:
                        after(dve, m_all, u)
                    for j in range(2):
                        idx = 2 * (s % KT) + j
                        dve.wait_ge(mx, 2 * a + j + 1)
                        dve.tensor_reduce(rmax[:, idx // KB, idx % KB:idx % KB + 1], ps[:, MX + j, :], AX_X, ALU.max).then_inc(md, 1)
                    if s % KT == KT - 1:
                        dve.wait_ge(md, 2 * a + 2)
                        after(dve, m_t, u)
                        dve.tensor_reduce(m8[:, :], rmax[:, :, :], AX_X, ALU.max).then_inc(m_all, 1)

                def negate(it, s):
                    if s % KT != 2:
                        return
                    v = 4 * it + s // KT
                    if isinstance(v, int) and (v == 0 or v > NU):
                        return
                    dve.wait_ge(m_t, v)
                    q = s // KT - 2
                    if q >= 0:
                        dve.wait_ge(m_in[q // UH], 16 * (UH * it + q % UH + 1))
                    dve.tensor_scalar(mrow[:, :], ps[0:QT, MISC, 0:P], -1.0, None, ALU.mult).then_inc(m_r, 1)

                def normalise(it, w):
                    par, uh = w // UH, w % UH
                    u = 4 * it + w + 1
                    dve.wait_ge(o_t, u)
                    after(dve, at_ok, u - 1)
                    o = ps[:, MISC, :].rearrange("p (c j d) -> p j c d", c=4, j=2)
                    r = rden[:, :].rearrange("p (j c) -> p j c", j=2)
                    dve.reciprocal(r, o[:, :, :, DK]).then_inc(den, 1)
                    dve.wait_ge(den, u)
                    if uh == 0:
                        after(dve, at_out[par], 16 * it)
                    for j in range(2):
                        ins = dve.tensor_tensor(att[:, par, uh * QT + 4 * j:uh * QT + 4 * j + 4, :], o[:, j, :, 0:DK],
                                                r[:, j, :].unsqueeze(2).broadcast_to([P, 4, DK]), ALU.mult)
                    ins.then_inc(at_ok, 1)

                def step(it, s):
                    maxima(it, s + AHEAD)
                    negate(it, s + AHEAD)
                    if s % KT == 4:
                        if s >= KT:
                            normalise(it, s // KT - 1)
                        elif not (isinstance(it, int) and it == 0):
                            normalise(it - 1, 3)

                for s in range(AHEAD):
                    maxima(0, s)
                    negate(0, s)
                sweep(dve, step)
                normalise(NHEAD // 2 - 1, 3)


def tail(nc, sb, sem, ps, wT, wfT, ctxT, ctxr, ident, fsc, fbi, x_t, att_t, out_t):
    ST = 6
    with ExitStack() as st:
        xr = sb("xr", [P, B, TB, D], F32, st)
        ai = sb("ai", [P, B, TB, D], F32, st)
        xh = sb("xh3", [P, B, TB, D], F32, st)
        xT = sb("xT3", [P, B, 2, CH, BLK], F16, st)
        y = sb("y", [P, B, TB, D], F32, st)
        gf = sb("gf", [T, B, BLK], F32, st)
        gT = sb("gT", [T, B, 2, BLK], F16, st)
        stat = sb("stat3", [P, TB, 6], F32, st)
        mv = sb("mv3", [P, TB, 2], F32, st)
        var = sb("var3", [P, TB], F32, st)
        std = sb("std3", [P, TB], F32, st)
        rstd = sb("rstd3", [P, TB], F32, st)
        x_in = [sem(f"x_in3{b}", st) for b in range(B)]
        a_in = [sem(f"a_in3{b}", st) for b in range(B)]
        turned = sem("turned3", st)
        xhi = sem("xhi3", st)
        xlo = sem("xlo3", st)
        tile = sem("tile3", st)
        taken = sem("taken3", st)
        stats = sem("stats3", st)
        aggr = sem("aggr3", st)
        var_ok = sem("var_ok3", st)
        std_ok = sem("std_ok3", st)
        rstd_ok = sem("rstd_ok3", st)
        normed = sem("normed3", st)
        h_ok = sem("h_ok", st)
        g_ok = sem("g_ok", st)
        ghi = sem("ghi", st)
        glo = sem("glo", st)
        biased = sem("biased", st)
        clipped = sem("clipped", st)
        final = sem("final", st)
        dve_passed = sem("dve_passed3", st)
        pool_passed = sem("pool_passed3", st)
        o_out = [sem(f"o_out{b}", st) for b in range(B)]
        N = S // BLK

        def loop(eng, body):
            body(0)
            with eng.Fori(1, N) as i:
                body(i)

        with nc.Block() as block:
            @block.sync
            def _(sp):
                def load(i):
                    for b in range(B):
                        n = B * i + b
                        after(sp, turned, CH * ST * (i - 1) + CH * (b + 1))
                        sp.dma_start(ai[:, b, :, :], att_t[b, i]).then_inc(a_in[b], 16)
                    for b in range(B):
                        n = B * i + b
                        after(sp, final, TB * (n - 1))
                        sp.dma_start(xr[:, b, :, :], x_t[b, i]).then_inc(x_in[b], 16)

                def store(i):
                    for b in range(B):
                        sp.wait_ge(final, TB * (B * i + b + 1))
                        sp.dma_start(out_t[b, i], y[:, b, :, :]).then_inc(o_out[b], 16)

                load(0)
                with sp.Fori(1, N) as i:
                    store(i - 1)
                    load(i)
                store(N - 1)
                for b in range(B):
                    sp.wait_ge(o_out[b], 16 * N)

            @block.tensor
            def _(pe):
                def turn(i, b, stage, src):
                    for c in range(CH):
                        g = CH * (ST * i + 2 * stage + b) + c
                        after(pe, xhi, g - 1)
                        after(pe, xlo, g - 1)
                        for t in range(TB):
                            ins = pe.transpose(ps[:, c % 2, t * P:(t + 1) * P], src[:, b, t, c * P:(c + 1) * P], ident[:, :])
                        ins.then_inc(turned, 1)

                def tiles(i, b, stage, terms):
                    for t in range(TB):
                        g = TB * (ST * i + 2 * stage + b) + t
                        after(pe, taken, g - TB + 1)
                        pairs = terms(t)
                        for k, (lhs, rhs) in enumerate(pairs):
                            ins = pe.matmul(ps[:, 2 + t, :], lhs, rhs, start=(k == 0), stop=(k == len(pairs) - 1))
                        ins.then_inc(tile, 1)

                def body(i):
                    for b in range(B):
                        pe.wait_ge(a_in[b], 16 * (i + 1))
                        turn(i, b, 0, ai)
                    for b in range(B):
                        pe.wait_ge(xlo, CH * (ST * i + b + 1))
                        tiles(i, b, 0, lambda t: [(xT[:, b, a, c, t * P:(t + 1) * P], wT["wo"][:, r, c, :])
                                                  for c in range(CH) for a, r in ((0, 0), (1, 0), (0, 1))])
                    for b in range(B):
                        pe.wait_ge(normed, TB * (4 * i + b + 1))
                        turn(i, b, 1, xh)
                        pe.wait_ge(xlo, CH * (ST * i + 2 + b + 1))
                        after(pe, g_ok, B * (i - 1) + b + 1)
                        k = 0
                        for c in range(CH):
                            for a, r in ((0, 0), (1, 0), (0, 1)):
                                ins = pe.matmul(ps[0:T, 6 + b, :], ctxT[:, b, a, c, :], xT[:, b, r, c, :],
                                                start=(k == 0), stop=(k == 3 * CH - 1))
                                k += 1
                        ins.then_inc(h_ok, 1)
                    for b in range(B):
                        pe.wait_ge(glo, B * i + b + 1)
                        tiles(i, b, 1, lambda t: [(gT[:, b, a, t * P:(t + 1) * P], ctxr[:, b, r, :])
                                                  for a, r in ((0, 0), (1, 0), (0, 1))])
                    for b in range(B):
                        pe.wait_ge(normed, TB * (4 * i + 2 + b + 1))
                        turn(i, b, 2, xh)
                        pe.wait_ge(xlo, CH * (ST * i + 4 + b + 1))
                        tiles(i, b, 2, lambda t: [(xT[:, b, a, c, t * P:(t + 1) * P], wfT[:, c, :])
                                                  for c in range(CH) for a in (0, 1)])

                loop(pe, body)

            @block.scalar
            def _(act):
                def high(i, b, stage):
                    for c in range(CH):
                        g = CH * (ST * i + 2 * stage + b) + c
                        act.wait_ge(turned, g + 1)
                        act.activation(xT[:, b, 0, c, :], ps[:, c % 2, :], ACT.Copy).then_inc(xhi, 1)

                def root(k):
                    act.wait_ge(var_ok, k + 1)
                    act.activation(std[:, :], var[:, :], ACT.Sqrt).then_inc(std_ok, 1)

                def body(i):
                    for b in range(B):
                        high(i, b, 0)
                    for b in range(B):
                        root(4 * i + b)
                    for b in range(B):
                        high(i, b, 1)
                    for b in range(B):
                        act.wait_ge(h_ok, B * i + b + 1)
                        after(act, glo, B * (i - 1) + b + 1)
                        act.activation(gf[:, b, :], ps[0:T, 6 + b, :], ACT.Gelu_apprx_tanh, scale=1.0 / WS).then_inc(g_ok, 1)
                        act.wait_ge(g_ok, B * i + b + 1)
                        act.activation(gT[:, b, 0, :], gf[:, b, :], ACT.Copy).then_inc(ghi, 1)
                    for b in range(B):
                        root(4 * i + 2 + b)
                    for b in range(B):
                        high(i, b, 2)

                loop(act, body)

            @block.vector
            def _(dve):
                def low(i, b, stage):
                    for c in range(CH):
                        g = CH * (ST * i + 2 * stage + b) + c
                        dve.wait_ge(xhi, g + 1)
                        dve.tensor_tensor(xT[:, b, 1, c, :], ps[:, c % 2, :], xT[:, b, 0, c, :], ALU.subtract).then_inc(xlo, 1)

                def add(i, b, stage):
                    for t in range(TB):
                        g = TB * (ST * i + 2 * stage + b) + t
                        dve.wait_ge(tile, g + 1)
                        dve.scalar_tensor_tensor(xr[:, b, t, :], ps[:, 2 + t, :], 1.0 / WS, xr[:, b, t, :],
                                                 ALU.mult, ALU.add).then_inc(taken, 1)

                def norm(i, b, stage, k):
                    dve.wait_ge(taken, TB * (ST * i + 2 * stage + b + 1))
                    for t in range(TB):
                        dve.bn_stats(stat[:, t, :], xr[:, b, t, :]).then_inc(stats, 1)
                    apart(dve, dve_passed, (stats, TB * (k + 1)), (normed, TB * k))
                    for t in range(TB):
                        dve.bn_aggr(mv[:, t, :], stat[:, t, :]).then_inc(aggr, 1)
                    dve.wait_ge(aggr, TB * (k + 1))
                    dve.tensor_scalar(var[:, :], mv[:, :, 1], EPS, None, ALU.add).then_inc(var_ok, 1)
                    dve.wait_ge(std_ok, k + 1)
                    dve.reciprocal(rstd[:, :], std[:, :]).then_inc(rstd_ok, 1)
                    dve.wait_ge(rstd_ok, k + 1)
                    after(dve, turned, CH * (ST * i + 2 + b + 1) if stage else CH * (ST * (i - 1) + 4 + b + 1))
                    for t in range(TB):
                        dve.tensor_scalar(xh[:, b, t, :], xr[:, b, t, :], mv[:, t, 0:1], rstd[:, t:t + 1],
                                          ALU.subtract, ALU.mult).then_inc(normed, 1)

                def body(i):
                    for b in range(B):
                        low(i, b, 0)
                    for b in range(B):
                        dve.wait_ge(x_in[b], 16 * (i + 1))
                        add(i, b, 0)
                        norm(i, b, 0, 4 * i + b)
                    for b in range(B):
                        low(i, b, 1)
                    for b in range(B):
                        dve.wait_ge(ghi, B * i + b + 1)
                        dve.tensor_tensor(gT[:, b, 1, :], gf[:, b, :], gT[:, b, 0, :], ALU.subtract).then_inc(glo, 1)
                    for b in range(B):
                        add(i, b, 1)
                        norm(i, b, 1, 4 * i + 2 + b)
                    for b in range(B):
                        low(i, b, 2)
                        after(dve, o_out[b], 16 * i)
                        for t in range(TB):
                            dve.wait_ge(tile, TB * (ST * i + 4 + b) + t + 1)
                            dve.tensor_tensor(y[:, b, t, :], ps[:, 2 + t, :], fsc[:, :], ALU.mult).then_inc(taken, 1)

                loop(dve, body)

            @block.gpsimd
            def _(pool):
                def body(i):
                    for b in range(B):
                        for t in range(TB):
                            g = TB * (B * i + b) + t
                            apart(pool, pool_passed, (taken, TB * (ST * i + 4 + b) + t + 1))
                            pool.tensor_tensor(y[:, b, t, :], y[:, b, t, :], fbi[:, :], ALU.add).then_inc(biased, 1)
                            apart(pool, pool_passed, (biased, g + 1))
                            pool.tensor_scalar(y[:, b, t, :], y[:, b, t, :], CLIP, -CLIP, ALU.min, ALU.max).then_inc(clipped, 1)
                            apart(pool, pool_passed, (clipped, g + 1))
                            pool.tensor_tensor(y[:, b, t, :], y[:, b, t, :], xr[:, b, t, :], ALU.add).then_inc(final, 1)

                loop(pool, body)


_INS = ["x", "ctx_1024", "L0_attn_W_q", "L0_attn_W_k", "L0_attn_W_v", "L0_attn_W_o",
        "L0_ffn_weights", "L0_ffn_scale", "L0_ffn_bias"]


def _constants():
    f = np.float32
    ident = np.eye(P, dtype=f)
    rot = np.zeros((P, P), f)
    even = np.arange(0, P, 2)
    rot[even + 1, even] = -1.0
    rot[even, even + 1] = 1.0
    inv_freq = f(1.0) / np.power(f(10000.0), np.arange(0, DK, 2, dtype=f) / f(DK)).astype(f)
    angle = (np.arange(S, dtype=f)[None, :] * inv_freq[(np.arange(P) % DK) // 2][:, None]).astype(f)
    return {"ident": ident, "rot": rot, "cos": np.cos(angle).astype(f), "sin": np.sin(angle).astype(f)}


def kernel(**inputs):
    import concourse.bacc as _bacc
    from concourse.bass_utils import run_bass_kernel_spmd as _run

    nc = _bacc.Bacc("TRN2", target_bir_lowering=False, num_devices=1)
    arrays, args = {}, []
    for name in _INS:
        a = np.ascontiguousarray(inputs[name])
        arrays[f"in_{name}"] = a
        args.append(nc.dram_tensor(f"in_{name}", a.shape, mybir.dt.from_np(a.dtype), kind="ExternalInput").ap())
    for name, a in _constants().items():
        arrays[f"const_{name}"] = a
        args.append(nc.dram_tensor(f"const_{name}", a.shape, mybir.dt.from_np(a.dtype), kind="ExternalInput").ap())
    args.append(nc.dram_tensor("out_0", (B, S, D), F32, kind="ExternalOutput").ap())
    decoder_layer(nc, *args)
    r = _run(nc, [arrays], core_ids=[0])
    return r.results[0]["out_0"]
```

```python
from contextlib import ExitStack

import numpy as np

import concourse.bass as bass
from concourse import mybir

F32 = mybir.dt.float32
F16 = mybir.dt.float16
ALU = mybir.AluOpType
ACT = mybir.ActivationFunctionType
AX_X = mybir.AxisListType.X

P = 128
B, S, D = 2, 2048, 512
H = 16
DK = D // H
T = 77
NTOK = B * S
CH = D // P
BLK = 512
TB = BLK // P
NBLK = NTOK // BLK
WS = 64.0
EPS = 1e-5
CLIP = 100.0
SM_SCALE = 1.0 / float(np.sqrt(np.float32(DK)))

KT = S // P
UQ = 1024
NU = B * H * S // UQ
NSTEP = NU * KT
SR = 3 * DK
MR = SR
AHEAD = 22
NP = 8
POOL_TILES = (0, 1, 3, 4, 6, 7, 9, 10, 12, 13)
TBLK = 256


def after(eng, sem, count):
    if isinstance(count, int) and count <= 0:
        return
    eng.wait_ge(sem, count)


def apart(eng, passed, *waits):
    for sem, c in waits:
        after(eng, sem, c)
    eng.sem_inc(passed)


def decoder_layer(nc, x, ctx_in, wq, wk, wv, wo, wf, fscale, fbias, ident_in, rot_in, cos_in, sin_in, out):
    r_scr = nc.dram_tensor("r_scr", (2, UQ), F32, kind="Internal").ap()
    q_scr = nc.dram_tensor("q_scr", (B, 2, D, S), F16, kind="Internal").ap()
    k_scr = nc.dram_tensor("k_scr", (B, 2, D, S), F16, kind="Internal").ap()
    att_scr = nc.dram_tensor("att_scr", (B, D, S), F32, kind="Internal").ap()
    x_t = x.rearrange("b (n t p) d -> b n p t d", t=TB, p=P)
    x_s = x.rearrange("b (n t p) d -> b n p t d", t=TBLK // P, p=P)
    out_s = out.rearrange("b (n t p) d -> b n p t d", t=TBLK // P, p=P)

    with ExitStack() as top:
        def sb(name, shape, dt, st=top):
            return st.enter_context(nc.sbuf_tensor(name, shape, dt))

        def sem(name, st=top):
            return st.enter_context(nc.semaphore(name))

        ps = top.enter_context(nc.psum_tensor("ps", [P, 8, 512], F32))
        wT = {m: sb(f"{m}T", [P, 2, CH, D], F16) for m in ("wq", "wk", "wv", "wo")}
        wfT = sb("wfT", [P, CH, D], F16)
        ctxT = sb("ctxT", [P, B, 2, CH, T], F16)
        ctxr = sb("ctxr", [T, B, 2, D], F16)
        ident = sb("ident", [P, P], F32)
        fsc = sb("fsc", [P, D], F32)
        fbi = sb("fbi", [P, D], F32)

        weights(nc, sb, sem, ps, wT, wfT, ctxT, ctxr, ident, fsc, fbi,
                ctx_in, wq, wk, wv, wo, wf, fscale, fbias, ident_in)
        with ExitStack() as mid:
            v_all = sb("v_all", [P, B * H, KT, DK], F32, mid)
            project(nc, sb, sem, ps, wT, ident, v_all, x_t, rot_in, cos_in, sin_in, q_scr, k_scr)
            attend(nc, sb, sem, ps, ident, v_all, q_scr, k_scr, r_scr, att_scr)
        tail(nc, sb, sem, ps, wT, wfT, ctxT, ctxr, ident, fsc, fbi, x_s, att_scr, out_s)


def weights(nc, sb, sem, ps, wT, wfT, ctxT, ctxr, ident, fsc, fbi,
            ctx_in, wq, wk, wv, wo, wf, fscale, fbias, ident_in):
    with ExitStack() as st:
        wraw = sb("wraw", [P, 5, CH, D], F32, st)
        craw = sb("craw", [T, B, D], F32, st)
        w_in = [sem(f"w_in{i}", st) for i in range(5)]
        c_in = sem("c_in", st)
        sc_in = sem("sc_in", st)
        id_in = sem("id_in", st)
        signed = sem("signed", st)
        turned = sem("turned", st)
        hi_done = sem("hi_done", st)
        lo_done = sem("lo_done", st)
        c_hi = sem("c_hi", st)
        NB = 8
        jobs = [(m, c) for m in range(4) for c in range(CH)] + [(4, c) for c in range(CH)] + [(5, b) for b in range(B)]
        mats = ("wq", "wk", "wv", "wo")
        los = [sum(1 for m, _ in jobs[:j + 1] if m != 4) for j in range(len(jobs))]

        def dst(j, half):
            m, c = jobs[j]
            if m < 4:
                return wT[mats[m]][:, half, c, :]
            if m == 4:
                return wfT[:, c, :]
            return ctxT[:, c, half, :, :]

        def src(j):
            if jobs[j][0] == 5:
                return ps[:, j % NB, :].rearrange("p (c t) -> p c t", c=CH)[:, :, 0:T]
            return ps[:, j % NB, :]

        with nc.Block() as block:
            @block.sync
            def _(sp):
                sp.dma_start(ident[:, :], ident_in).then_inc(id_in, 16)
                for i, w in enumerate((wq, wk, wv, wo, wf)):
                    sp.dma_start(wraw[:, i, :, :], w.rearrange("(o p) i -> p o i", p=P)).then_inc(w_in[i], 16)
                sp.dma_start(craw[:, :, :], ctx_in.rearrange("b t d -> t b d")).then_inc(c_in, 16)
                sp.dma_start(fsc[:, :], fscale.rearrange("(a d) -> a d", a=1).broadcast_to([P, D])).then_inc(sc_in, 16)
                sp.dma_start(fbi[:, :], fbias.rearrange("(a d) -> a d", a=1).broadcast_to([P, D])).then_inc(sc_in, 16)
                sp.wait_ge(sc_in, 32)

            @block.tensor
            def _(pe):
                pe.wait_ge(id_in, 16)
                for j, (m, c) in enumerate(jobs):
                    if c == 0:
                        if m == 4:
                            pe.wait_ge(signed, 1)
                        elif m == 5:
                            pe.wait_ge(c_in, 16)
                        else:
                            pe.wait_ge(w_in[m], 16)
                    if j >= NB:
                        pe.wait_ge(hi_done, j - NB + 1)
                        pe.wait_ge(lo_done, los[j - NB])
                    for o in range(CH):
                        if m == 5:
                            ins = pe.transpose(ps[:, j % NB, o * P:o * P + T], craw[:, c, o * P:(o + 1) * P], ident[0:T, 0:T])
                        else:
                            ins = pe.transpose(ps[:, j % NB, o * P:(o + 1) * P], wraw[:, m, o, c * P:(c + 1) * P], ident[:, :])
                    ins.then_inc(turned, 1)

            @block.scalar
            def _(act):
                for j, (m, _) in enumerate(jobs):
                    act.wait_ge(turned, j + 1)
                    act.activation(dst(j, 0), src(j), ACT.Copy, scale=1.0 if m == 4 else WS).then_inc(hi_done, 1)
                for b in range(B):
                    act.activation(ctxr[:, b, 0, :], craw[:, b, :], ACT.Copy, scale=WS).then_inc(c_hi, 1)

            @block.vector
            def _(dve):
                dve.wait_ge(w_in[4], 16)
                dve.tensor_scalar(wraw[:, 4, :, :], wraw[:, 4, :, :], 0.0, 0.5, ALU.is_ge, ALU.subtract).then_inc(signed, 1)
                for j, (m, _) in enumerate(jobs):
                    if m != 4:
                        dve.wait_ge(hi_done, j + 1)
                        dve.scalar_tensor_tensor(dst(j, 1), src(j), WS, dst(j, 0), ALU.mult, ALU.subtract).then_inc(lo_done, 1)
                for b in range(B):
                    dve.wait_ge(c_hi, b + 1)
                    dve.scalar_tensor_tensor(ctxr[:, b, 1, :], craw[:, b, :], WS, ctxr[:, b, 0, :], ALU.mult, ALU.subtract)
                dve.wait_ge(sc_in, 32)
                dve.tensor_scalar(fsc[:, :], fsc[:, :], 2.0, None, ALU.mult)


def project(nc, sb, sem, ps, wT, ident, v_all, x_t, rot_in, cos_in, sin_in, q_scr, k_scr):
    NT = 2 * CH
    with ExitStack() as st:
        rot = sb("rot", [P, P], F32, st)
        cos = sb("cos", [P, S], F32, st)
        sin = sb("sin", [P, S], F32, st)
        xin = sb("xin", [P, 2, TB, D], F32, st)
        xh = sb("xh", [P, TB, D], F32, st)
        xT = sb("xT", [P, 2, 2, CH, BLK], F16, st)
        stat = sb("stat", [P, TB, 6], F32, st)
        mv = sb("mv", [P, TB, 2], F32, st)
        var = sb("var", [P, TB], F32, st)
        std = sb("std", [P, TB], F32, st)
        rstd = sb("rstd", [P, TB], F32, st)
        raw = sb("raw", [P, 2, BLK], F32, st)
        rs = sb("rs", [P, 2, BLK], F32, st)
        rc = sb("rc", [P, 2, BLK], F32, st)
        ro = sb("ro", [P, 2, BLK], F32, st)
        pair = sb("pair", [P, 2, 2, BLK], F16, st)
        tab_in = sem("tab_in", st)
        x_in = [sem(f"x_in{i}", st) for i in range(2)]
        stats = sem("stats", st)
        aggr = sem("aggr", st)
        var_ok = sem("var_ok", st)
        std_ok = sem("std_ok", st)
        rstd_ok = sem("rstd_ok", st)
        normed = sem("normed", st)
        turned = sem("turned1", st)
        xhi = sem("xhi", st)
        xlo = sem("xlo", st)
        proj = sem("proj", st)
        raw_ok = sem("raw_ok", st)
        rot_ok = sem("rot_ok", st)
        rs_ok = sem("rs_ok", st)
        rc_ok = sem("rc_ok", st)
        ro_ok = sem("ro_ok", st)
        phi = sem("phi", st)
        plo = sem("plo", st)
        stored = [sem(f"stored{i}", st) for i in range(2)]
        vps = sem("vps", st)
        v_ok = sem("v_ok", st)
        dve_passed = sem("dve_passed", st)
        pool_passed = sem("pool_passed", st)

        def loop(eng, body):
            for b in range(B):
                body(0, b)
            with eng.Fori(1, NBLK // 2) as i:
                for b in range(B):
                    body(i, b)

        with nc.Block() as block:
            @block.sync
            def _(sp):
                sp.dma_start(cos[:, :], cos_in).then_inc(tab_in, 16)
                sp.dma_start(sin[:, :], sin_in).then_inc(tab_in, 16)
                sp.dma_start(rot[:, :], rot_in).then_inc(tab_in, 16)
                for b in range(B):
                    sp.dma_start(xin[:, b, :, :], x_t[b, 0]).then_inc(x_in[b], 16)

                def body(i, b):
                    n = 2 * i + b
                    for o in range(NT):
                        g = NT * n + o
                        scr = q_scr if o < CH else k_scr
                        c = o % CH
                        for half, ok in ((0, phi), (1, plo)):
                            sp.wait_ge(ok, g + 1)
                            sp.dma_start(scr[b, half, c * P:(c + 1) * P, bass.ds(i * BLK, BLK)],
                                         pair[:, o % 2, half, :]).then_inc(stored[o % 2], 16)

                def load(i, b):
                    n = 2 * i + b
                    sp.wait_ge(normed, TB * (n - 1))
                    sp.dma_start(xin[:, b, :, :], x_t[b, i]).then_inc(x_in[b], 16)

                with sp.Fori(0, NBLK // 2 - 1) as i:
                    for b in range(B):
                        load(i + 1, b)
                        body(i, b)
                for b in range(B):
                    body(NBLK // 2 - 1, b)
                for o in range(2):
                    sp.wait_ge(stored[o], 16 * NT * NBLK)

            @block.vector
            def _(dve):
                dve.wait_ge(tab_in, 48)

                def norm(i, b):
                    n = 2 * i + b
                    dve.wait_ge(x_in[b], 16 * (i + 1))
                    for t in range(TB):
                        dve.bn_stats(stat[:, t, :], xin[:, b, t, :]).then_inc(stats, 1)
                    apart(dve, dve_passed, (stats, TB * (n + 1)))
                    for t in range(TB):
                        dve.bn_aggr(mv[:, t, :], stat[:, t, :]).then_inc(aggr, 1)
                    dve.wait_ge(aggr, TB * (n + 1))
                    dve.tensor_scalar(var[:, :], mv[:, :, 1], EPS, None, ALU.add).then_inc(var_ok, 1)
                    dve.wait_ge(std_ok, n + 1)
                    dve.reciprocal(rstd[:, :], std[:, :]).then_inc(rstd_ok, 1)
                    dve.wait_ge(rstd_ok, n + 1)
                    after(dve, turned, CH * n)
                    for t in range(TB):
                        dve.tensor_scalar(xh[:, t, :], xin[:, b, t, :], mv[:, t, 0:1], rstd[:, t:t + 1],
                                          ALU.subtract, ALU.mult).then_inc(normed, 1)

                def low(i, b):
                    n = 2 * i + b
                    for c in range(CH):
                        dve.wait_ge(xhi, CH * n + c + 1)
                        dve.tensor_tensor(xT[:, b, 1, c, :], ps[:, c % 2, :], xT[:, b, 0, c, :], ALU.subtract).then_inc(xlo, 1)

                def rope(i, b):
                    n = 2 * i + b
                    for o in range(NT + 1):
                        if o < NT:
                            g = NT * n + o
                            dve.wait_ge(rot_ok, g + 1)
                            after(dve, ro_ok, g - 1)
                            dve.tensor_tensor(rs[:, o % 2, :], ps[:, 4 + o % 2, :], sin[:, bass.ds(i * BLK, BLK)],
                                              ALU.mult).then_inc(rs_ok, 1)
                            dve.wait_ge(rs_ok, g + 1)
                            dve.wait_ge(rc_ok, g + 1)
                            after(dve, phi, g - 1)
                            after(dve, plo, g - 1)
                            dve.tensor_tensor(ro[:, o % 2, :], rs[:, o % 2, :], rc[:, o % 2, :], ALU.add).then_inc(ro_ok, 1)
                        if o >= 1:
                            g = NT * n + o - 1
                            dve.wait_ge(phi, g + 1)
                            dve.tensor_tensor(pair[:, (o - 1) % 2, 1, :], ro[:, (o - 1) % 2, :], pair[:, (o - 1) % 2, 0, :],
                                              ALU.subtract).then_inc(plo, 1)

                norm(0, 0)
                low(0, 0)
                norm(0, 1)
                low(0, 1)
                rope(0, 0)
                with dve.Fori(1, NBLK // 2) as i:
                    norm(i, 0)
                    low(i, 0)
                    rope(i - 1, 1)
                    norm(i, 1)
                    low(i, 1)
                    rope(i, 0)
                rope(NBLK // 2 - 1, 1)

            @block.tensor
            def _(pe):
                pe.wait_ge(tab_in, 48)

                def turn(i, b):
                    n = 2 * i + b
                    pe.wait_ge(normed, TB * (n + 1))
                    for c in range(CH):
                        g = CH * n + c
                        after(pe, xhi, g - 1)
                        after(pe, xlo, g - 1)
                        for t in range(TB):
                            ins = pe.transpose(ps[:, c % 2, t * P:(t + 1) * P], xh[:, t, c * P:(c + 1) * P], ident[:, :])
                        ins.then_inc(turned, 1)

                def three(dst, lhs, rhs):
                    k = 0
                    for c in range(CH):
                        for a, r in ((0, 0), (0, 1), (1, 0)):
                            ins = pe.matmul(dst, lhs(a, c), rhs(r, c), start=(k == 0), stop=(k == 3 * CH - 1))
                            k += 1
                    return ins

                def rotate(g, o):
                    pe.wait_ge(raw_ok, g + 1)
                    after(pe, rs_ok, g - 1)
                    pe.matmul(ps[:, 4 + o % 2, :], rot[:, :], raw[:, o % 2, :], start=True, stop=True).then_inc(rot_ok, 1)

                def multiply(i, b):
                    n = 2 * i + b
                    pe.wait_ge(xlo, CH * (n + 1))
                    for o in range(NT):
                        g = NT * n + o
                        w = wT["wq" if o < CH else "wk"]
                        c0 = (o % CH) * P
                        after(pe, raw_ok, g - 1)
                        three(ps[:, 2 + o % 2, :], lambda a, c: w[:, a, c, c0:c0 + P],
                              lambda r, c: xT[:, b, r, c, :]).then_inc(proj, 1)
                        if o >= 1:
                            rotate(g - 1, o - 1)
                    for t in range(TB):
                        g = TB * n + t
                        after(pe, v_ok, g - 1)
                        three(ps[:, 6 + t % 2, :], lambda a, c: xT[:, b, a, c, t * P:(t + 1) * P],
                              lambda r, c: wT["wv"][:, r, c, :]).then_inc(vps, 1)
                        if t == 0:
                            rotate(NT * (n + 1) - 1, NT - 1)

                turn(0, 0)
                turn(0, 1)
                multiply(0, 0)
                with pe.Fori(1, NBLK // 2) as i:
                    turn(i, 0)
                    multiply(i - 1, 1)
                    turn(i, 1)
                    multiply(i, 0)
                multiply(NBLK // 2 - 1, 1)

            @block.scalar
            def _(act):
                def high(i, b):
                    n = 2 * i + b
                    act.wait_ge(var_ok, n + 1)
                    act.activation(std[:, :], var[:, :], ACT.Sqrt).then_inc(std_ok, 1)
                    after(act, vps, TB * (n - 1))
                    for c in range(CH):
                        act.wait_ge(turned, CH * n + c + 1)
                        act.activation(xT[:, b, 0, c, :], ps[:, c % 2, :], ACT.Copy).then_inc(xhi, 1)

                def split(g, o):
                    act.wait_ge(ro_ok, g + 1)
                    if not (isinstance(g, int) and g < 2):
                        act.wait_ge(stored[o % 2], 16 * (g - o % 2))
                    act.activation(pair[:, o % 2, 0, :], ro[:, o % 2, :], ACT.Copy).then_inc(phi, 1)

                def evacuate(i, b):
                    n = 2 * i + b
                    for o in range(NT):
                        g = NT * n + o
                        act.wait_ge(proj, g + 1)
                        after(act, rot_ok, g - 1)
                        after(act, rc_ok, g - 1)
                        act.activation(raw[:, o % 2, :], ps[:, 2 + o % 2, :], ACT.Copy, scale=1.0 / WS).then_inc(raw_ok, 1)
                        if o >= 2:
                            split(g - 2, o - 2)
                    for t in range(TB):
                        act.wait_ge(vps, TB * n + t + 1)
                        act.activation(v_all[:, b * H:(b + 1) * H, i * TB + t, :],
                                       ps[:, 6 + t % 2, :].rearrange("p (h d) -> p h d", h=H), ACT.Copy, scale=1.0 / WS).then_inc(v_ok, 1)
                        if t < 2:
                            split(NT * (n + 1) - 2 + t, NT - 2 + t)

                high(0, 0)
                high(0, 1)
                evacuate(0, 0)
                with act.Fori(1, NBLK // 2) as i:
                    high(i, 0)
                    evacuate(i - 1, 1)
                    high(i, 1)
                    evacuate(i, 0)
                evacuate(NBLK // 2 - 1, 1)

            @block.gpsimd
            def _(pool):
                pool.wait_ge(tab_in, 48)

                def body(i, b):
                    n = 2 * i + b
                    for o in range(NT):
                        g = NT * n + o
                        apart(pool, pool_passed, (raw_ok, g + 1), (ro_ok, g - 1))
                        pool.tensor_tensor(rc[:, o % 2, :], raw[:, o % 2, :], cos[:, bass.ds(i * BLK, BLK)],
                                           ALU.mult).then_inc(rc_ok, 1)
                loop(pool, body)


def attend(nc, sb, sem, ps, ident, v_all, q_scr, k_scr, r_scr, att_scr):
    UH = S // UQ
    QT = UQ // P
    KB = S // 512
    HS = UH * KT
    QB = UQ // 4
    NPA = len(POOL_TILES) - 1
    ITER = 2 * HS
    NHEAD = B * H
    UNITS = ITER // KT
    with ExitStack() as st:
        qs = sb("qs", [MR + 1, 2, S], F16, st)
        ks = sb("ks", [MR + 1, 2, S], F16, st)
        vh = sb("vh", [P, 2, KT, DK], F32, st)
        ones = sb("ones", [P, DK], F32, st)
        psum_p = sb("psum_p", [P, 2, UQ], F32, st)
        pr = sb("pr", [P, NP, UQ], F32, st)
        rmax = sb("rmax", [P, QT, KB], F32, st)
        m8 = sb("m8", [P, QT], F32, st)
        mrow = sb("mrow", [QT, P], F16, st)
        od = sb("od", [P, 2, 2 * QB], F32, st)
        d8 = sb("d8", [P, UQ // P], F32, st)
        r8 = sb("r8", [P, UQ // P], F32, st)
        rb = sb("rb", [P, QB], F32, st)
        on = sb("on", [P, QB], F32, st)
        qk_in = [sem(f"qk_in{i}", st) for i in range(2)]
        init = sem("init", st)
        v_copied = sem("v_copied", st)
        sc = sem("sc", st)
        ex = sem("ex", st)
        pv = sem("pv", st)
        mx = sem("mx", st)
        md = sem("md", st)
        m_all = sem("m_all", st)
        m_t = sem("m_t", st)
        m_r = sem("m_r", st)
        m_in = [sem(f"m_in{i}", st) for i in range(2)]
        ps_p = sem("ps_p", st)
        rs_all = sem("rs_all", st)
        od_ok = sem("od_ok", st)
        d8_in = sem("d8_in", st)
        r8_ok = sem("r8_ok", st)
        r8_out = sem("r8_out", st)
        rb_in = sem("rb_in", st)
        on_ok = sem("on_ok", st)
        at_out = sem("at_out", st)
        passed = sem("passed", st)

        SC, MX, OV, MISC = 0, 4, 6, 7

        def head_of(s):
            return (s // HS) % 2

        def sweep(eng, step):
            for s in range(ITER):
                step(0, s)
            with eng.Fori(1, NHEAD // 2 - 1) as it:
                for s in range(ITER):
                    step(it, s)
            for s in range(ITER):
                step(NHEAD // 2 - 1, s)

        def exists(it, s):
            return not (isinstance(it, int) and ITER * it + s >= NSTEP)

        def adds(tiles, it, s):
            upto = sum(1 for k in tiles if k <= s % KT)
            return (len(tiles) - 1) * (UNITS * it + s // KT) + (max(1, upto - 1) if upto else 0)

        with nc.Block() as block:
            @block.gpsimd
            def _(pool):
                pool.memset(ones[:, :], 1.0).then_inc(init, 1)
                pool.wait_ge(init, 1)
                pool.memset(ks[MR:MR + 1, :, :], 1.0).then_inc(init, 1)
                pool.wait_ge(init, 2)

                def step(it, s):
                    k, u = s % KT, UNITS * it + s // KT
                    if k in POOL_TILES[1:]:
                        n = POOL_TILES.index(k)
                        pool.wait_ge(ex, ITER * it + s + 1)
                        acc = psum_p[:, (s // KT) % 2, :]
                        if n == 1:
                            after(pool, rs_all, u - 1)
                            first = pr[:, (s - k + POOL_TILES[0]) % NP, :]
                        else:
                            after(pool, ps_p, NPA * u + n - 1)
                            first = acc
                        pool.tensor_tensor(acc, first, pr[:, s % NP, :], ALU.add).then_inc(ps_p, 1)

                sweep(pool, step)

            @block.sync
            def _(sp):
                def load(b, i, par):
                    d0 = (2 * i + par) * DK
                    for r, half in enumerate((0, 1, 0)):
                        sp.dma_start(qs[r * DK:(r + 1) * DK, par, :], q_scr[b, half, bass.ds(d0, DK), :]).then_inc(qk_in[par], 16)
                    for r, half in enumerate((0, 0, 1)):
                        sp.dma_start(ks[r * DK:(r + 1) * DK, par, :], k_scr[b, half, bass.ds(d0, DK), :]).then_inc(qk_in[par], 16)

                def store_max(v):
                    it, w = v
                    u = 4 * it + w
                    par, uh = w // UH, w % UH
                    sp.wait_ge(m_r, u + 1)
                    sp.dma_start(qs[MR:MR + 1, par, uh * UQ:(uh + 1) * UQ], mrow[:, :]).then_inc(m_in[par], 16)

                def invert(u, p):
                    sp.wait_ge(od_ok, u + 1)
                    sp.dma_start(d8[:, :], od[0:P:DK, p, QB:2 * QB]).then_inc(d8_in, 16)
                    sp.wait_ge(r8_ok, u + 1)
                    sp.dma_start(r_scr[p].rearrange("(p e) -> p e", p=P), r8[:, :]).then_inc(r8_out, 16)
                    sp.wait_ge(r8_out, 16 * (u + 1))
                    for j in range(4):
                        sp.dma_start(rb[j * DK:(j + 1) * DK, :],
                                     r_scr[p:p + 1, j * QB:(j + 1) * QB].broadcast_to([DK, QB])).then_inc(rb_in, 16)

                def store_att(b, i, w):
                    u = UNITS * (H // 2 * b + i) + w
                    par, uh = w // UH, w % UH
                    invert(u, w % 2)
                    sp.wait_ge(on_ok, u + 1)
                    for j in range(4):
                        q0 = uh * UQ + j * QB
                        sp.dma_start(att_scr[b, bass.ds((2 * i + par) * DK, DK), q0:q0 + QB],
                                     on[j * DK:(j + 1) * DK, :]).then_inc(at_out, 16)

                load(0, 0, 0)
                load(0, 0, 1)
                store_max((0, 0))
                def heads(b, i, last):
                    base = H // 2 * b + i
                    nb, ni = (b + 1, 0) if isinstance(i, int) and i + 1 == H // 2 else (b, i + 1)
                    store_max((base, 1))
                    store_att(b, i, 0)
                    store_max((base, 2))
                    if not last:
                        sp.wait_ge(sc, ITER * base + HS)
                        load(nb, ni, 0)
                    store_att(b, i, 1)
                    store_max((base, 3))
                    store_att(b, i, 2)
                    if not last:
                        store_max((base + 1, 0))
                        sp.wait_ge(sc, ITER * base + 2 * HS)
                        load(nb, ni, 1)
                    store_att(b, i, 3)

                for b in range(B):
                    with sp.Fori(0, H // 2 - 1) as i:
                        heads(b, i, False)
                    heads(b, H // 2 - 1, b == B - 1)
                sp.wait_ge(at_out, 64 * NU)

            @block.tensor
            def _(pe):
                pe.wait_ge(init, 2)

                def maxima(it, s):
                    if not exists(it, s):
                        return
                    a = ITER * it + s
                    par, uh, k = head_of(s), (s // KT) % UH, s % KT
                    if s % HS == 0:
                        pe.wait_ge(qk_in[par], 96 * (it + 1 + (0 if s < ITER else 1)))
                    for j in range(2):
                        idx = 2 * k + j
                        qt, kb = idx // KB, idx % KB
                        after(pe, md, 2 * a + j - 1)
                        q0 = uh * UQ + qt * P
                        pe.matmul(ps[:, MX + j, :], qs[0:SR, par, q0:q0 + P], ks[0:SR, par, kb * 512:(kb + 1) * 512],
                                  start=True, stop=True).then_inc(mx, 1)

                def turn_max(it, s):
                    if s % KT != 1:
                        return
                    v = 4 * it + s // KT
                    if isinstance(v, int) and (v == 0 or v > NU):
                        return
                    pe.wait_ge(m_all, v)
                    after(pe, m_r, v - 1)
                    pe.transpose(ps[0:QT, MISC, 0:P], m8[:, :], ident[:, :]).then_inc(m_t, 1)

                def scores(it, s):
                    g = ITER * it + s
                    par, uh, k = head_of(s), (s // KT) % UH, s % KT
                    if k == 0:
                        pe.wait_ge(m_in[par], 16 * (UH * it + uh + 1))
                    after(pe, ex, g - 1)
                    for j in range(2):
                        q0 = uh * UQ + j * 512
                        ins = pe.matmul(ps[:, SC + 2 * (s % 2) + j, :], ks[:, par, k * P:(k + 1) * P], qs[:, par, q0:q0 + 512],
                                        start=True, stop=True)
                    ins.then_inc(sc, 1)

                def values(it, s):
                    g = ITER * it + s
                    par, k = head_of(s), s % KT
                    if s % HS == 0:
                        pe.wait_ge(v_copied, 2 * it + par + 1)
                    if k == 0:
                        after(pe, od_ok, UNITS * it + s // KT)
                    pe.wait_ge(ex, g + 1)
                    for j in range(4):
                        ins = pe.matmul(ps[DK * j:DK * j + DK, OV, 0:QB], vh[:, par, k, :], pr[:, s % NP, j * QB:(j + 1) * QB],
                                        start=(k == 0), stop=(k == KT - 1), skip_group_check=True,
                                        tile_position=(0, DK * j))
                    if k not in POOL_TILES:
                        ins = row_sums(pr[:, s % NP, :])
                    ins.then_inc(pv, 1)
                    up = (s // KT) % 2
                    if k == KT - 1:
                        pe.wait_ge(ps_p, adds(POOL_TILES, it, s))
                        row_sums(psum_p[:, up, :]).then_inc(rs_all, 1)

                def row_sums(p):
                    for j in range(4):
                        ins = pe.matmul(ps[DK * j:DK * j + DK, OV, QB:2 * QB], ones[:, :], p[:, j * QB:(j + 1) * QB],
                                        start=False, stop=False, skip_group_check=True, tile_position=(0, DK * j))
                    return ins

                def step(it, s):
                    scores(it, s)
                    sa = s + AHEAD
                    maxima(it, sa)
                    turn_max(it, sa)
                    if s >= 1:
                        values(it, s - 1)
                    elif not (isinstance(it, int) and it == 0):
                        values(it - 1, ITER - 1)

                for s in range(AHEAD):
                    maxima(0, s)
                    turn_max(0, s)
                sweep(pe, step)
                values(NHEAD // 2 - 1, ITER - 1)

            @block.scalar
            def _(act):
                def evacuate(u, p):
                    act.wait_ge(rs_all, u)
                    after(act, on_ok, u - 2)
                    act.activation(od[:, p, :], ps[:, OV, :], ACT.Copy).then_inc(od_ok, 1)

                def copy(it, par):
                    apart(act, passed, (pv, HS * (2 * it + par - 1)))
                    act.activation(vh[:, par, :, :], v_all[:, 2 * it + par, :, :], ACT.Copy).then_inc(v_copied, 1)

                def step(it, s):
                    g = ITER * it + s
                    act.wait_ge(sc, g + 1)
                    after(act, pv, g - NP + 1)
                    if (s - NP) % KT in POOL_TILES:
                        after(act, ps_p, adds(POOL_TILES, it, s - NP))
                    act.activation(pr[:, s % NP, :], ps[:, SC + 2 * (s % 2):SC + 2 * (s % 2) + 2, :].rearrange("p a n -> p (a n)"),
                                   ACT.Exp, scale=SM_SCALE).then_inc(ex, 1)
                    if s % KT == 0 and not (isinstance(it, int) and g == 0):
                        evacuate(UNITS * it + s // KT, (s // KT - 1) % 2)
                    if s % HS == 11:
                        if s < HS:
                            copy(it, 1)
                        elif not (isinstance(it, int) and it == NHEAD // 2 - 1):
                            copy(it + 1, 0)

                copy(0, 0)
                sweep(act, step)
                evacuate(NU, 1)

            @block.vector
            def _(dve):
                def maxima(it, s):
                    if not exists(it, s):
                        return
                    a = ITER * it + s
                    u = 4 * it + s // KT
                    if s % KT == 0:
                        after(dve, m_all, u)
                    for j in range(2):
                        idx = 2 * (s % KT) + j
                        dve.wait_ge(mx, 2 * a + j + 1)
                        dve.tensor_reduce(rmax[:, idx // KB, idx % KB:idx % KB + 1], ps[:, MX + j, :], AX_X, ALU.max).then_inc(md, 1)
                    if s % KT == KT - 1:
                        dve.wait_ge(md, 2 * a + 2)
                        after(dve, m_t, u)
                        dve.tensor_reduce(m8[:, :], rmax[:, :, :], AX_X, ALU.max).then_inc(m_all, 1)

                def negate(it, s):
                    if s % KT != 2:
                        return
                    v = 4 * it + s // KT
                    if isinstance(v, int) and (v == 0 or v > NU):
                        return
                    dve.wait_ge(m_t, v)
                    q = s // KT - 2
                    if q >= 0:
                        dve.wait_ge(m_in[q // UH], 16 * (UH * it + q % UH + 1))
                    dve.tensor_scalar(mrow[:, :], ps[0:QT, MISC, 0:P], -1.0, None, ALU.mult).then_inc(m_r, 1)

                def invert(it, w):
                    u = UNITS * it + w + 1
                    dve.wait_ge(d8_in, 16 * u)
                    after(dve, r8_out, 16 * (u - 1))
                    dve.reciprocal(r8[:, :], d8[:, :]).then_inc(r8_ok, 1)

                def normalise(it, w):
                    u = UNITS * it + w + 1
                    dve.wait_ge(rb_in, 64 * u)
                    after(dve, at_out, 64 * (u - 1))
                    dve.tensor_tensor(on[:, :], od[:, w % 2, 0:QB], rb[:, :], ALU.mult).then_inc(on_ok, 1)

                def step(it, s):
                    maxima(it, s + AHEAD)
                    negate(it, s + AHEAD)
                    for at, do in ((5, invert), (9, normalise)):
                        if s % KT == at:
                            if s >= KT:
                                do(it, s // KT - 1)
                            elif not (isinstance(it, int) and it == 0):
                                do(it - 1, UNITS - 1)

                for s in range(AHEAD):
                    maxima(0, s)
                    negate(0, s)
                sweep(dve, step)
                invert(NHEAD // 2 - 1, 3)
                normalise(NHEAD // 2 - 1, 3)


def tail(nc, sb, sem, ps, wT, wfT, ctxT, ctxr, ident, fsc, fbi, x_s, att_scr, out_s):
    TT = TBLK // P
    NB = NTOK // TBLK
    G = 4
    HC = CH // 2
    with ExitStack() as st:
        xin = sb("xin3", [P, 2, TT, D], F32, st)
        xr = sb("xr", [P, G, TT, D], F32, st)
        aT = sb("aT", [P, 2, CH, TBLK], F32, st)
        aP = sb("aP", [P, 2, 2, CH, TBLK], F16, st)
        xh1 = sb("xh1", [P, TT, D], F32, st)
        xh2 = sb("xh2", [P, TT, D], F32, st)
        xT1 = sb("xT1", [P, 2, CH, TBLK], F16, st)
        xT2 = sb("xT2", [P, 2, CH, TBLK], F16, st)
        gf = sb("gf", [T, TBLK], F32, st)
        gT = sb("gT", [T, 2, TBLK], F16, st)
        y = sb("y", [P, 2, TT, D], F32, st)
        stat = sb("stat3", [P, 2, TT, 6], F32, st)
        mv = sb("mv3", [P, 2, TT, 2], F32, st)
        var = sb("var3", [P, 2, TT], F32, st)
        std = sb("std3", [P, 2, TT], F32, st)
        rstd = sb("rstd3", [P, 2, TT], F32, st)
        x_in = [sem(f"x_in3{p}", st) for p in range(2)]
        a_in = [sem(f"a_in3{p}", st) for p in range(2)]
        o_out = [sem(f"o_out{p}", st) for p in range(2)]
        a_hi, a_lo = sem("a_hi", st), sem("a_lo", st)
        turned = {g: sem(f"turned_{g}", st) for g in "BD"}
        t_hi = {g: sem(f"t_hi_{g}", st) for g in "BD"}
        t_lo = {g: sem(f"t_lo_{g}", st) for g in "BD"}
        tile = {g: sem(f"tile_{g}", st) for g in "ACD"}
        taken = {g: sem(f"taken_{g}", st) for g in "ACD"}
        h_ok, g_ok, g_hi, g_lo = sem("h_ok", st), sem("g_ok", st), sem("g_hi", st), sem("g_lo", st)
        stats = [sem(f"stats3{k}", st) for k in range(2)]
        aggr = [sem(f"aggr3{k}", st) for k in range(2)]
        var_ok = [sem(f"var_ok3{k}", st) for k in range(2)]
        std_ok = [sem(f"std_ok3{k}", st) for k in range(2)]
        rstd_ok = [sem(f"rstd_ok3{k}", st) for k in range(2)]
        normed = [sem(f"normed3{k}", st) for k in range(2)]
        biased, clipped, final = sem("biased", st), sem("clipped", st), sem("final", st)
        dve_passed, pool_passed = sem("dve_passed3", st), sem("pool_passed3", st)
        A_BANK, C_BANK, D_BANK, H_BANK = 6, 4, 4, 0
        T_BANK = {"D": 0, "B": 2}
        SPLITS = ((0, 0), (1, 0), (0, 1))

        class Slot:

            def __init__(self, k, r):
                self.k, self.r = k, r

            def block(self, off):
                k, r = self.k, self.r - off
                m = G * k + r
                if isinstance(m, int) and not 0 <= m < NB:
                    return None
                return m, r % 2, 2 * k + r // 2, r % G

        def slots(eng, body):
            for r in range(G):
                body(Slot(0, r))
            with eng.Fori(1, NB // G - 1) as k:
                for r in range(G):
                    body(Slot(k, r))
            for r in range(G + 3):
                body(Slot(NB // G - 1, r))

        with nc.Block() as block:
            @block.sync
            def _(sp):
                def load_attention(sl, off):
                    if blk := sl.block(off):
                        m, b, i, _ = blk
                        after(sp, a_hi, m - 1)
                        after(sp, a_lo, m - 1)
                        sp.dma_start(aT[:, b, :, :], att_scr[b].rearrange("(c p) s -> p c s", p=P)[:, :, bass.ds(i * TBLK, TBLK)])\
                            .then_inc(a_in[b], 16)

                def load_x(sl, off):
                    if blk := sl.block(off):
                        m, b, i, _ = blk
                        after(sp, taken["A"], TT * (m - 1))
                        sp.dma_start(xin[:, b, :, :], x_s[b, i]).then_inc(x_in[b], 16)

                def store(sl):
                    if blk := sl.block(3):
                        m, b, i, _ = blk
                        sp.wait_ge(final, TT * (m + 1))
                        sp.dma_start(out_s[b, i], y[:, b, :, :]).then_inc(o_out[b], 16)

                def body(sl):
                    load_attention(sl, -2)
                    load_x(sl, -2)
                    store(sl)

                for r in range(2):
                    load_attention(Slot(0, r), 0)
                    load_x(Slot(0, r), 0)
                slots(sp, body)
                for b in range(2):
                    sp.wait_ge(o_out[b], 16 * NB // 2)

            @block.tensor
            def _(pe):
                def turn(g, sl, off, src, k):
                    if not (blk := sl.block(off)):
                        return
                    m = blk[0]
                    pe.wait_ge(normed[k], TT * (m + 1))
                    if g == "D":
                        pe.wait_ge(g_ok, min(m + 2, NB) if isinstance(m, int) else m + 2)
                    after(pe, t_lo[g], HC * m)
                    for c in range(CH):
                        for t in range(TT):
                            o = (c % 2) * TBLK + t * P
                            ins = pe.transpose(ps[:, T_BANK[g] + c // 2, o:o + P], src[:, t, c * P:(c + 1) * P], ident[:, :])
                        if c % 2:
                            ins.then_inc(turned[g], 1)

                def tiles(g, bank, m, terms):
                    for t in range(TT):
                        pairs = terms(t)
                        for k, (lhs, rhs) in enumerate(pairs):
                            ins = pe.matmul(ps[:, bank + t, :], lhs, rhs, start=(k == 0), stop=(k == len(pairs) - 1))
                        ins.then_inc(tile[g], 1)

                def body(sl):
                    turn("D", sl, 3, xh2, 1)
                    turn("B", sl, 1, xh1, 0)
                    if blk := sl.block(2):
                        m, b = blk[:2]
                        pe.wait_ge(g_lo, m + 1)
                        after(pe, taken["D"], TT * (m - 1))
                        tiles("C", C_BANK, m, lambda t: [(gT[:, a, t * P:(t + 1) * P], ctxr[:, b, r, :]) for a, r in SPLITS])
                    if blk := sl.block(0):
                        m, b = blk[:2]
                        pe.wait_ge(a_lo, m + 1)
                        after(pe, taken["A"], TT * m)
                        tiles("A", A_BANK, m, lambda t: [(aP[:, b, a, c, t * P:(t + 1) * P], wT["wo"][:, r, c, :])
                                                         for c in range(CH) for a, r in SPLITS])
                    if blk := sl.block(3):
                        m = blk[0]
                        pe.wait_ge(t_lo["D"], HC * (m + 1))
                        pe.wait_ge(taken["C"], TT * min(m + 2, NB) if isinstance(m, int) else TT * (m + 2))
                        tiles("D", D_BANK, m, lambda t: [(xT2[:, a, c, t * P:(t + 1) * P], wfT[:, c, :])
                                                         for c in range(CH) for a in (0, 1)])
                    if blk := sl.block(1):
                        m, b = blk[:2]
                        pe.wait_ge(t_lo["B"], HC * (m + 1))
                        after(pe, t_lo["D"], HC * (m - 1))
                        after(pe, g_ok, m)
                        n = 0
                        for c in range(CH):
                            for a, r in SPLITS:
                                ins = pe.matmul(ps[0:T, H_BANK, 0:TBLK], ctxT[:, b, a, c, :], xT1[:, r, c, :],
                                                start=(n == 0), stop=(n == 3 * CH - 1))
                                n += 1
                        ins.then_inc(h_ok, 1)

                slots(pe, body)

            @block.scalar
            def _(act):
                def attention(sl, off):
                    if not (blk := sl.block(off)):
                        return
                    m, b, i, _ = blk
                    act.wait_ge(a_in[b], 16 * (i + 1))
                    after(act, tile["A"], TT * (m - 1))
                    act.activation(aP[:, b, 0, :, :], aT[:, b, :, :], ACT.Copy).then_inc(a_hi, 1)

                def high(g, sl, off, dst):
                    if not (blk := sl.block(off)):
                        return
                    for c in range(HC):
                        act.wait_ge(turned[g], HC * blk[0] + c + 1)
                        act.activation(dst[:, 0, 2 * c:2 * c + 2, :], ps[:, T_BANK[g] + c, :].rearrange("p (a t) -> p a t", a=2),
                                       ACT.Copy).then_inc(t_hi[g], 1)

                def root(k, sl, off):
                    if not (blk := sl.block(off)):
                        return
                    act.wait_ge(var_ok[k], blk[0] + 1)
                    act.activation(std[:, k, :], var[:, k, :], ACT.Sqrt).then_inc(std_ok[k], 1)

                def body(sl):
                    high("D", sl, 3, xT2)
                    high("B", sl, 1, xT1)
                    root(1, sl, 2)
                    attention(sl, -1)
                    root(0, sl, 0)
                    if blk := sl.block(1):
                        m = blk[0]
                        act.wait_ge(h_ok, m + 1)
                        after(act, g_lo, m)
                        act.activation(gf[:, :], ps[0:T, H_BANK, 0:TBLK], ACT.Gelu_apprx_tanh, scale=1.0 / WS).then_inc(g_ok, 1)
                        act.wait_ge(g_ok, m + 1)
                        act.activation(gT[:, 0, :], gf[:, :], ACT.Copy).then_inc(g_hi, 1)

                attention(Slot(0, 0), 0)
                slots(act, body)

            @block.vector
            def _(dve):
                def low(g, sl, off, dst):
                    if not (blk := sl.block(off)):
                        return
                    for c in range(HC):
                        dve.wait_ge(t_hi[g], HC * blk[0] + c + 1)
                        dve.tensor_tensor(dst[:, 1, 2 * c:2 * c + 2, :], ps[:, T_BANK[g] + c, :].rearrange("p (a t) -> p a t", a=2),
                                          dst[:, 0, 2 * c:2 * c + 2, :], ALU.subtract).then_inc(t_lo[g], 1)

                def norm(k, g, m, ring, dst, turned_g):
                    dve.wait_ge(taken[g], TT * (m + 1))
                    for t in range(TT):
                        dve.bn_stats(stat[:, k, t, :], xr[:, ring, t, :]).then_inc(stats[k], 1)
                    apart(dve, dve_passed, (stats[k], TT * (m + 1)), (normed[k], TT * m))
                    for t in range(TT):
                        dve.bn_aggr(mv[:, k, t, :], stat[:, k, t, :]).then_inc(aggr[k], 1)
                    dve.wait_ge(aggr[k], TT * (m + 1))
                    dve.tensor_scalar(var[:, k, :], mv[:, k, :, 1], EPS, None, ALU.add).then_inc(var_ok[k], 1)
                    dve.wait_ge(std_ok[k], m + 1)
                    dve.reciprocal(rstd[:, k, :], std[:, k, :]).then_inc(rstd_ok[k], 1)
                    dve.wait_ge(rstd_ok[k], m + 1)
                    after(dve, turned[turned_g], HC * m)
                    for t in range(TT):
                        dve.tensor_scalar(dst[:, t, :], xr[:, ring, t, :], mv[:, k, t, 0:1], rstd[:, k, t:t + 1],
                                          ALU.subtract, ALU.mult).then_inc(normed[k], 1)

                def body(sl):
                    low("D", sl, 3, xT2)
                    low("B", sl, 1, xT1)
                    if blk := sl.block(2):
                        m, b, i, ring = blk
                        for t in range(TT):
                            dve.wait_ge(tile["C"], TT * m + t + 1)
                            dve.scalar_tensor_tensor(xr[:, ring, t, :], ps[:, C_BANK + t, :], 1.0 / WS, xr[:, ring, t, :],
                                                     ALU.mult, ALU.add).then_inc(taken["C"], 1)
                        norm(1, "C", m, ring, xh2, "D")
                    if blk := sl.block(0):
                        m, b, i, ring = blk
                        dve.wait_ge(x_in[b], 16 * (i + 1))
                        after(dve, final, TT * (m - G + 1))
                        for t in range(TT):
                            dve.wait_ge(tile["A"], TT * m + t + 1)
                            dve.scalar_tensor_tensor(xr[:, ring, t, :], ps[:, A_BANK + t, :], 1.0 / WS, xin[:, b, t, :],
                                                     ALU.mult, ALU.add).then_inc(taken["A"], 1)
                        norm(0, "A", m, ring, xh1, "B")
                    if blk := sl.block(3):
                        m, b, i, _ = blk
                        after(dve, o_out[b], 16 * i)
                        for t in range(TT):
                            dve.wait_ge(tile["D"], TT * m + t + 1)
                            dve.tensor_tensor(y[:, b, t, :], ps[:, D_BANK + t, :], fsc[:, :], ALU.mult).then_inc(taken["D"], 1)
                    if blk := sl.block(1):
                        dve.wait_ge(g_hi, blk[0] + 1)
                        dve.tensor_tensor(gT[:, 1, :], gf[:, :], gT[:, 0, :], ALU.subtract).then_inc(g_lo, 1)

                slots(dve, body)

            @block.gpsimd
            def _(pool):
                def attention(sl, off):
                    if not (blk := sl.block(off)):
                        return
                    m, b = blk[:2]
                    pool.wait_ge(a_hi, m + 1)
                    pool.tensor_tensor(aP[:, b, 1, :, :], aT[:, b, :, :], aP[:, b, 0, :, :], ALU.subtract).then_inc(a_lo, 1)

                def body(sl):
                    attention(sl, -1)
                    if blk := sl.block(3):
                        m, b, i, ring = blk
                        for t in range(TT):
                            n = TT * m + t
                            pool.wait_ge(taken["D"], n + 1)
                            pool.tensor_tensor(y[:, b, t, :], y[:, b, t, :], fbi[:, :], ALU.add).then_inc(biased, 1)
                            apart(pool, pool_passed, (biased, n + 1))
                            pool.tensor_scalar(y[:, b, t, :], y[:, b, t, :], CLIP, -CLIP, ALU.min, ALU.max).then_inc(clipped, 1)
                            pool.wait_ge(clipped, n + 1)
                            pool.tensor_tensor(y[:, b, t, :], y[:, b, t, :], xr[:, ring, t, :], ALU.add).then_inc(final, 1)

                attention(Slot(0, 0), 0)
                slots(pool, body)

_INS = ["x", "ctx_1024", "L0_attn_W_q", "L0_attn_W_k", "L0_attn_W_v", "L0_attn_W_o",
        "L0_ffn_weights", "L0_ffn_scale", "L0_ffn_bias"]


def _constants():
    f = np.float32
    ident = np.eye(P, dtype=f)
    rot = np.zeros((P, P), f)
    even = np.arange(0, P, 2)
    rot[even + 1, even] = -1.0
    rot[even, even + 1] = 1.0
    inv_freq = f(1.0) / np.power(f(10000.0), np.arange(0, DK, 2, dtype=f) / f(DK)).astype(f)
    angle = (np.arange(S, dtype=f)[None, :] * inv_freq[(np.arange(P) % DK) // 2][:, None]).astype(f)
    return {"ident": ident, "rot": rot, "cos": np.cos(angle).astype(f), "sin": np.sin(angle).astype(f)}


def kernel(**inputs):
    import concourse.bacc as _bacc
    from concourse.bass_utils import run_bass_kernel_spmd as _run

    nc = _bacc.Bacc("TRN2", target_bir_lowering=False, num_devices=1)
    arrays, args = {}, []
    for name in _INS:
        a = np.ascontiguousarray(inputs[name])
        arrays[f"in_{name}"] = a
        args.append(nc.dram_tensor(f"in_{name}", a.shape, mybir.dt.from_np(a.dtype), kind="ExternalInput").ap())
    for name, a in _constants().items():
        arrays[f"const_{name}"] = a
        args.append(nc.dram_tensor(f"const_{name}", a.shape, mybir.dt.from_np(a.dtype), kind="ExternalInput").ap())
    args.append(nc.dram_tensor("out_0", (B, S, D), F32, kind="ExternalOutput").ap())
    decoder_layer(nc, *args)
    r = _run(nc, [arrays], core_ids=[0])
    return r.results[0]["out_0"]
```

```python
from contextlib import ExitStack

import numpy as np

import concourse.bass as bass
from concourse import mybir

F32 = mybir.dt.float32
F16 = mybir.dt.float16
ALU = mybir.AluOpType
ACT = mybir.ActivationFunctionType
AX_X = mybir.AxisListType.X

P = 128
B, S, D = 2, 2048, 512
H = 16
DK = D // H
T = 77
NTOK = B * S
CH = D // P
BLK = 512
TB = BLK // P
NBLK = NTOK // BLK
WS = 64.0
EPS = 1e-5
CLIP = 100.0
SM_SCALE = 1.0 / float(np.sqrt(np.float32(DK)))

KT = S // P
UQ = 1024
NU = B * H * S // UQ
NSTEP = NU * KT
SR = 3 * DK
MR = SR
AHEAD = 24
NP = 8
POOL_TILES = (0, 1, 3, 4, 6, 7, 9, 10, 12, 13, 15)
UH = S // UQ
QT = UQ // P
KB = S // 512
HS = UH * KT
ITER = 2 * HS
UNITS = ITER // KT
QB = UQ // 4
TBLK = 256


def after(eng, sem, count):
    if isinstance(count, int) and count <= 0:
        return
    eng.wait_ge(sem, count)


def apart(eng, passed, *waits):
    for sem, c in waits:
        after(eng, sem, c)
    eng.sem_inc(passed)


def decoder_layer(nc, x, ctx_in, wq, wk, wv, wo, wf, fscale, fbias, ident_in, cos_in, sin_in, out):
    r_scr = nc.dram_tensor("r_scr", (2, UQ), F32, kind="Internal").ap()
    q_scr = nc.dram_tensor("q_scr", (B, 2, D, S), F16, kind="Internal").ap()
    k_scr = nc.dram_tensor("k_scr", (B, 2, D, S), F16, kind="Internal").ap()
    att_scr = nc.dram_tensor("att_scr", (D, NTOK), F32, kind="Internal").ap()
    x_t = x.rearrange("b (n t p) d -> b n p t d", t=TB, p=P)
    x_s = x.rearrange("b (n t p) d -> b n p t d", t=TBLK // P, p=P)
    out_s = out.rearrange("b (n t p) d -> b n p t d", t=TBLK // P, p=P)

    with ExitStack() as top:
        def sb(name, shape, dt, st=top):
            return st.enter_context(nc.sbuf_tensor(name, shape, dt))

        def sem(name, st=top):
            return st.enter_context(nc.semaphore(name))

        ps = top.enter_context(nc.psum_tensor("ps", [P, 8, 512], F32))
        ident = sb("ident", [P, P], F32)
        v_all = sb("v_all", [P, B * H, KT, DK], F32)
        nrm = Normaliser(sb, sem, r_scr, att_scr, top)
        mxs = Maxima(sb, sem, ps, ident, q_scr, k_scr, nrm.sum_ok, top)
        project(nc, sb, sem, ps, ident, v_all, mxs, x_t, (wq, wk, wv), ident_in, cos_in, sin_in, q_scr, k_scr)
        wT = {"wo": sb("woT", [P, 2, CH, D], F16)}
        wfT = sb("wfT", [P, CH, D], F16)
        ctxT = sb("ctxT", [P, B, 2, CH, T], F16)
        ctxr = sb("ctxr", [T, B, 2, D], F16)
        fsc = sb("fsc", [P, D], F32)
        fbi = sb("fbi", [P, D], F32)
        late = LateWeights(sb, sem, ps, wT, wfT, ctxT, ctxr, ident, fsc, fbi, ctx_in, wo, wf, fscale, fbias, top)
        inputs = TailInputs(sb, sem, x_s, att_scr, top)
        attend(nc, sb, sem, ps, v_all, mxs, nrm, late, inputs.first)
        tail(nc, sb, sem, ps, wT, wfT, ctxT, ctxr, ident, fsc, fbi, inputs, nrm, out_s)


class Weights:
    BANKS = (2, 3, 4, 5, 6, 7)

    def __init__(self, sb, sem, ps, ident, raw, dram, st):
        self.T = [sb(f"w{m}T", [P, 2, CH, D], F16, st) for m in "qkv"]
        self.ps, self.ident, self.raw, self.dram = ps, ident, raw, dram
        self.w_in = [sem(f"w_in{i}", st) for i in range(3)]
        self.turned = sem("w_turned", st)
        self.hi_done = sem("w_hi", st)
        self.lo_done = sem("w_lo", st)

    def in_order(self, m, a, pattern):
        return a.rearrange(pattern, e=2) if m < 2 else a

    def dst(self, m, c, half):
        return self.in_order(m, self.T[m][:, half, c, :], "p (e r) -> p e r")

    def src(self, m, c):
        return self.in_order(m, self.ps[:, self.bank(m, c), :], "p (r e) -> p e r")

    def bank(self, m, c):
        return self.BANKS[(CH * m + c) % len(self.BANKS)]

    def load(self, sp, m):
        sp.dma_start(self.raw[m], self.dram[m].rearrange("(o p) i -> p o i", p=P)).then_inc(self.w_in[m], 16)

    def turn(self, pe, m):
        pe.wait_ge(self.w_in[m], 16)
        for c in range(CH):
            j = CH * m + c
            after(pe, self.hi_done, j - len(self.BANKS) + 1)
            after(pe, self.lo_done, j - len(self.BANKS) + 1)
            for o in range(CH):
                ins = pe.transpose(self.ps[:, self.bank(m, c), o * P:(o + 1) * P], self.raw[m][:, o, c * P:(c + 1) * P],
                                   self.ident[:, :])
            ins.then_inc(self.turned, 1)

    def high(self, act, m):
        for c in range(CH):
            act.wait_ge(self.turned, CH * m + c + 1)
            act.activation(self.dst(m, c, 0), self.src(m, c), ACT.Copy, scale=WS).then_inc(self.hi_done, 1)

    def low(self, dve, m):
        for c in range(CH):
            dve.wait_ge(self.hi_done, CH * m + c + 1)
            dve.scalar_tensor_tensor(self.dst(m, c, 1), self.src(m, c), WS, self.dst(m, c, 0), ALU.mult, ALU.subtract)\
                .then_inc(self.lo_done, 1)


class LateWeights:

    def __init__(self, sb, sem, ps, wT, wfT, ctxT, ctxr, ident, fsc, fbi, ctx_in, wo, wf, fscale, fbias, st):
        self.ps, self.wT, self.wfT, self.ctxT, self.ctxr, self.ident = ps, wT, wfT, ctxT, ctxr, ident
        self.fsc, self.fbi = fsc, fbi
        self.ctx_in, self.w_dram, self.fscale, self.fbias = ctx_in, (wo, wf), fscale, fbias
        self.sb, self.st = sb, st
        self.w_in = [sem(f"late_w_in{i}", st) for i in range(2)]
        self.c_in, self.sc_in = sem("c_in", st), sem("sc_in", st)
        self.signed = sem("signed", st)
        self.turned = sem("late_turned", st)
        self.hi_done, self.lo_done = sem("late_hi", st), sem("late_lo", st)
        self.c_hi = sem("c_hi", st)
        self.jobs = [("wo", c) for c in range(CH)] + [("ctx", b) for b in range(B)] + [("wf", c) for c in range(CH)]
        self.banks = [b for i, b in enumerate(Maxima.BANKS) if i != Maxima.TURN_AT % 3]

    def buffers(self, st):
        self.wraw = self.sb("late_wraw", [P, 2, CH, D], F32, st)
        self.craw = self.sb("craw", [T, B, D], F32, st)

    def bank(self, j):
        return self.banks[j % len(self.banks)]

    def dst(self, j, half):
        m, c = self.jobs[j]
        if m == "wo":
            return self.wT["wo"][:, half, c, :]
        if m == "wf":
            return self.wfT[:, c, :]
        return self.ctxT[:, c, half, :, :]

    def src(self, j):
        bank = self.ps[:, self.bank(j), :]
        return bank.rearrange("p (c t) -> p c t", c=CH)[:, :, 0:T] if self.jobs[j][0] == "ctx" else bank

    def load(self, sp):
        for i, w in enumerate(self.w_dram):
            sp.dma_start(self.wraw[:, i, :, :], w.rearrange("(o p) i -> p o i", p=P)).then_inc(self.w_in[i], 16)
        sp.dma_start(self.craw[:, :, :], self.ctx_in.rearrange("b t d -> t b d")).then_inc(self.c_in, 16)
        for t, w in ((self.fsc, self.fscale), (self.fbi, self.fbias)):
            sp.dma_start(t[:, :], w.rearrange("(a d) -> a d", a=1).broadcast_to([P, D])).then_inc(self.sc_in, 16)

    def turn(self, pe, j):
        m, c = self.jobs[j]
        if j == 0:
            pe.wait_ge(self.w_in[0], 16)
        elif m == "ctx":
            pe.wait_ge(self.c_in, 16)
        elif m == "wf":
            pe.wait_ge(self.signed, 1)
        last = j - len(self.banks)
        after(pe, self.hi_done, last + 1)
        after(pe, self.lo_done, min(last, CH + B - 1) + 1)
        for o in range(CH):
            if m == "ctx":
                ins = pe.transpose(self.ps[:, self.bank(j), o * P:o * P + T], self.craw[:, c, o * P:(o + 1) * P], self.ident[0:T, 0:T])
            else:
                ins = pe.transpose(self.ps[:, self.bank(j), o * P:(o + 1) * P],
                                   self.wraw[:, 0 if m == "wo" else 1, o, c * P:(c + 1) * P], self.ident[:, :])
        ins.then_inc(self.turned, 1)

    def high(self, act, j):
        act.wait_ge(self.turned, j + 1)
        act.activation(self.dst(j, 0), self.src(j), ACT.Copy, scale=1.0 if self.jobs[j][0] == "wf" else WS).then_inc(self.hi_done, 1)

    def low(self, dve, j):
        if self.jobs[j][0] != "wf":
            dve.wait_ge(self.hi_done, j + 1)
            dve.scalar_tensor_tensor(self.dst(j, 1), self.src(j), WS, self.dst(j, 0), ALU.mult, ALU.subtract).then_inc(self.lo_done, 1)

    def ctx_high(self, act):
        act.wait_ge(self.c_in, 16)
        for b in range(B):
            act.activation(self.ctxr[:, b, 0, :], self.craw[:, b, :], ACT.Copy, scale=WS).then_inc(self.c_hi, 1)

    def early(self, dve):
        dve.wait_ge(self.w_in[1], 16)
        dve.tensor_scalar(self.wraw[:, 1, :, :], self.wraw[:, 1, :, :], 0.0, 0.5, ALU.is_ge, ALU.subtract).then_inc(self.signed, 1)
        for b in range(B):
            dve.wait_ge(self.c_hi, b + 1)
            dve.scalar_tensor_tensor(self.ctxr[:, b, 1, :], self.craw[:, b, :], WS, self.ctxr[:, b, 0, :], ALU.mult, ALU.subtract)
        dve.wait_ge(self.sc_in, 32)
        dve.tensor_scalar(self.fsc[:, :], self.fsc[:, :], 2.0, None, ALU.mult)


def project(nc, sb, sem, ps, ident, v_all, mxs, x_t, w_dram, ident_in, cos_in, sin_in, q_scr, k_scr):
    NT = 2 * CH
    with ExitStack() as st:
        cos = sb("cos", [P, S], F32, st)
        sin = sb("sin", [P, S], F32, st)
        xin = sb("xin", [P, 2, TB, D], F32, st)
        xh = sb("xh", [P, TB, D], F32, st)
        xT = sb("xT", [P, 2, 2, CH, BLK], F16, st)
        stat = sb("stat", [P, TB, 6], F32, st)
        mv = sb("mv", [P, TB, 2], F32, st)
        var = sb("var", [P, TB], F32, st)
        std = sb("std", [P, TB], F32, st)
        rstd = sb("rstd", [P, TB], F32, st)
        raw = sb("raw", [P, 4, BLK], F32, st)
        prod = sb("prod", [P, 2, 4, BLK], F32, st)
        EC, OS, OC, ES = range(4)
        wt = Weights(sb, sem, ps, ident, (prod[:, 0, :, :], prod[:, 1, :, :], raw[:, :, :]), w_dram, st)
        id_in = sem("id_in", st)
        tab_in = sem("tab_in", st)
        x_in = [sem(f"x_in{i}", st) for i in range(2)]
        pair = sb("pair", [P, 2, 2, BLK], F16, st)
        stats = sem("stats", st)
        aggr = sem("aggr", st)
        var_ok = sem("var_ok", st)
        std_ok = sem("std_ok", st)
        rstd_ok = sem("rstd_ok", st)
        normed = sem("normed", st)
        turned = sem("turned1", st)
        xhi = sem("xhi", st)
        xlo = sem("xlo", st)
        proj = sem("proj", st)
        raw_ok = sem("raw_ok", st)
        ec_ok = sem("ec_ok", st)
        prod_ok = sem("prod_ok", st)
        ro_ok = sem("ro_ok", st)
        phi = sem("phi", st)
        plo = sem("plo", st)
        stored = [sem(f"stored{i}", st) for i in range(2)]
        vps = sem("vps", st)
        v_ok = sem("v_ok", st)
        dve_passed = sem("dve_passed", st)
        pool_passed = sem("pool_passed", st)

        def columns(o):
            return o // CH, (o % 2) * (D // 2) + (o % CH) // 2 * P

        def v_bank(t, last):
            return t % 2 if last else 6 + t % 2

        def beside(o, k):
            s = 2 * (o - 2) + k // 2
            return [(s, k % 2)] if 0 <= s < AHEAD else []

        TILES = NT + TB
        REST = range(TILES, AHEAD // 2 + 2)

        def loop(eng, body):
            for b in range(B):
                body(0, b)
            with eng.Fori(1, NBLK // 2) as i:
                for b in range(B):
                    body(i, b)

        with nc.Block() as block:
            @block.sync
            def _(sp):
                sp.dma_start(ident[:, :], ident_in).then_inc(id_in, 16)
                wt.load(sp, 0)
                sp.dma_start(xin[:, 0, :, :], x_t[0, 0]).then_inc(x_in[0], 16)
                wt.load(sp, 1)
                sp.dma_start(xin[:, 1, :, :], x_t[1, 0]).then_inc(x_in[1], 16)
                wt.load(sp, 2)
                sp.dma_start(cos[:, :], cos_in).then_inc(tab_in, 16)
                sp.dma_start(sin[:, :], sin_in).then_inc(tab_in, 16)

                def body(i, b):
                    n = 2 * i + b
                    for o in range(NT):
                        g = NT * n + o
                        m, c0 = columns(o)
                        scr = (q_scr, k_scr)[m]
                        for half, ok in ((0, phi), (1, plo)):
                            sp.wait_ge(ok, g + 1)
                            sp.dma_start(scr[b, half, c0:c0 + P, bass.ds(i * BLK, BLK)],
                                         pair[:, o % 2, half, :]).then_inc(stored[o % 2], 16)

                def load(i, b):
                    n = 2 * i + b
                    sp.wait_ge(normed, TB * (n - 1))
                    sp.dma_start(xin[:, b, :, :], x_t[b, i]).then_inc(x_in[b], 16)

                with sp.Fori(0, NBLK // 2 - 1) as i:
                    for b in range(B):
                        load(i + 1, b)
                        body(i, b)
                body(NBLK // 2 - 1, 0)
                for o in range(2):
                    sp.wait_ge(stored[o], 16 * NT * (NBLK - 1))
                mxs.load(sp, 0, 0, 0)
                mxs.load(sp, 0, 0, 1)
                body(NBLK // 2 - 1, 1)
                mxs.store_max(sp, (0, 0))
                sp.wait_ge(mxs.m_in[0], 16)
                for o in range(2):
                    sp.wait_ge(stored[o], 16 * NT * NBLK)

            @block.vector
            def _(dve):
                def statistics(i, b, t):
                    dve.wait_ge(x_in[b], 16 * (i + 1))
                    dve.bn_stats(stat[:, t, :], xin[:, b, t, :]).then_inc(stats, 1)

                def variance(i, b):
                    n = 2 * i + b
                    apart(dve, dve_passed, (stats, TB * (n + 1)))
                    for t in range(TB):
                        dve.bn_aggr(mv[:, t, :], stat[:, t, :]).then_inc(aggr, 1)
                    dve.wait_ge(aggr, TB * (n + 1))
                    dve.tensor_scalar(var[:, :], mv[:, :, 1], EPS, None, ALU.add).then_inc(var_ok, 1)

                def inverse(i, b):
                    n = 2 * i + b
                    dve.wait_ge(std_ok, n + 1)
                    dve.reciprocal(rstd[:, :], std[:, :]).then_inc(rstd_ok, 1)

                def normalise(i, b, t):
                    n = 2 * i + b
                    dve.wait_ge(rstd_ok, n + 1)
                    after(dve, turned, CH * n)
                    dve.tensor_scalar(xh[:, t, :], xin[:, b, t, :], mv[:, t, 0:1], rstd[:, t:t + 1],
                                      ALU.subtract, ALU.mult).then_inc(normed, 1)

                norm_steps = [[lambda i, b, t=t: statistics(i, b, t)] for t in range(TB)] + [[variance], [], [inverse]] \
                    + [[lambda i, b, t=t: normalise(i, b, t)] for t in range(TB)]

                def norm(i, b):
                    for steps in norm_steps:
                        for do in steps:
                            do(i, b)

                def low(i, b):
                    n = 2 * i + b
                    for c in range(CH):
                        dve.wait_ge(xhi, CH * n + c + 1)
                        dve.tensor_tensor(xT[:, b, 1, c, :], ps[:, c % 2, :], xT[:, b, 0, c, :], ALU.subtract).then_inc(xlo, 1)

                def rope(i, b, following, last=False):
                    n = 2 * i + b
                    for o in range(NT + 3):
                        done = 0
                        if o % 2 == 0 and o < NT:
                            g, q = NT * n + o, NT // 2 * n + o // 2
                            dve.wait_ge(raw_ok, g + 1)
                            after(dve, phi, g - 3)
                            after(dve, plo, g - 3)
                            dve.tensor_tensor(prod[:, o // 2 % 2, EC, :], raw[:, o % 4, :], cos[:, bass.ds(i * BLK, BLK)],
                                              ALU.mult).then_inc(ec_ok, 1)
                            if last:
                                first_maxima(o, done)
                                done += 1
                        if 2 <= o < NT + 2:
                            r = o - 2
                            q, e = NT // 2 * n + r // 2, r % 2
                            into, other = ((EC, OS), (OC, ES))[e]
                            if not e:
                                dve.wait_ge(ec_ok, q + 1)
                            dve.wait_ge(prod_ok, 3 * q + 2 + e)
                            dve.tensor_tensor(prod[:, r // 2 % 2, into, :], prod[:, r // 2 % 2, into, :], prod[:, r // 2 % 2, other, :],
                                              ALU.add if e else ALU.subtract).then_inc(ro_ok, 1)
                            if last:
                                first_maxima(o, done)
                                done += 1
                        if o >= 3:
                            r = o - 3
                            dve.wait_ge(phi, NT * n + r + 1)
                            dve.tensor_tensor(pair[:, r % 2, 1, :], prod[:, r // 2 % 2, (EC, OC)[r % 2], :], pair[:, r % 2, 0, :],
                                              ALU.subtract).then_inc(plo, 1)
                        if following:
                            for do in norm_steps[o]:
                                do(*following)
                        if last:
                            for k in range(done, 4):
                                first_maxima(o, k)

                def first_maxima(o, k):
                    for s, j in beside(o, k):
                        mxs.reduce(dve, 0, s, j)
                        if j == 1:
                            mxs.negate(dve, 0, s)

                wt.low(dve, 0)
                norm(0, 0)
                low(0, 0)
                wt.low(dve, 1)
                norm(0, 1)
                low(0, 1)
                wt.low(dve, 2)
                dve.wait_ge(tab_in, 32)
                rope(0, 0, (1, 0))

                def two(i, last):
                    low(i, 0)
                    rope(i - 1, 1, (i, 1))
                    low(i, 1)
                    rope(i, 0, None if last else (i + 1, 0))

                with dve.Fori(1, NBLK // 2 - 1) as i:
                    two(i, False)
                two(NBLK // 2 - 1, True)
                rope(NBLK // 2 - 1, 1, None, True)
                for o in (*range(NT + 3, TILES), *REST):
                    for k in range(4):
                        first_maxima(o, k)

            @block.tensor
            def _(pe):
                def turn(i, b):
                    n = 2 * i + b
                    pe.wait_ge(normed, TB * (n + 1))
                    for c in range(CH):
                        g = CH * n + c
                        after(pe, xhi, g - 1)
                        after(pe, xlo, g - 1)
                        for t in range(TB):
                            ins = pe.transpose(ps[:, c % 2, t * P:(t + 1) * P], xh[:, t, c * P:(c + 1) * P], ident[:, :])
                        ins.then_inc(turned, 1)

                def three(dst, lhs, rhs, between=None):
                    k = 0
                    for c in range(CH):
                        for a, r in ((0, 0), (0, 1), (1, 0)):
                            ins = pe.matmul(dst, lhs(a, c), rhs(r, c), start=(k == 0), stop=(k == 3 * CH - 1))
                            k += 1
                        if between and c < CH - 1:
                            between(c)
                    return ins

                def multiply(i, b, last=False):
                    n = 2 * i + b

                    def between(o):
                        return (lambda c: first_maxima(o, c)) if last else None

                    pe.wait_ge(xlo, CH * (n + 1))
                    for o in range(NT):
                        g = NT * n + o
                        m, c0 = columns(o)
                        w = wt.T[m]
                        after(pe, raw_ok, g - 1)
                        three(ps[:, 2 + o % 2, :], lambda a, c: w[:, a, c, c0:c0 + P],
                              lambda r, c: xT[:, b, r, c, :], between(o)).then_inc(proj, 1)
                        if last:
                            between(o)(CH - 1)
                    for t in range(TB):
                        g = TB * n + t
                        after(pe, v_ok, g - 1)
                        three(ps[:, v_bank(t, last), :], lambda a, c: xT[:, b, a, c, t * P:(t + 1) * P],
                              lambda r, c: wt.T[2][:, r, c, :], between(NT + t)).then_inc(vps, 1)
                        if last:
                            between(NT + t)(CH - 1)

                def first_maxima(o, k):
                    for s, j in beside(o, k):
                        if s == 0 and j == 0:
                            pe.wait_ge(v_ok, TB * (NBLK - 1))
                        mxs.scores(pe, 0, s, j)
                        if j == 1:
                            mxs.turn_max(pe, 0, s)

                pe.wait_ge(id_in, 16)
                wt.turn(pe, 0)
                turn(0, 0)
                wt.turn(pe, 1)
                turn(0, 1)
                wt.turn(pe, 2)
                pe.wait_ge(wt.hi_done, 3 * CH)
                pe.wait_ge(wt.lo_done, 3 * CH)
                multiply(0, 0)
                with pe.Fori(1, NBLK // 2) as i:
                    turn(i, 0)
                    multiply(i - 1, 1)
                    turn(i, 1)
                    multiply(i, 0)
                multiply(NBLK // 2 - 1, 1, True)
                for o in REST:
                    for k in range(4):
                        first_maxima(o, k)

            @block.scalar
            def _(act):
                def root(i, b):
                    n = 2 * i + b
                    act.wait_ge(var_ok, n + 1)
                    act.activation(std[:, :], var[:, :], ACT.Sqrt).then_inc(std_ok, 1)

                def high(i, b):
                    n = 2 * i + b
                    after(act, vps, TB * (n - 1))
                    for c in range(CH):
                        act.wait_ge(turned, CH * n + c + 1)
                        act.activation(xT[:, b, 0, c, :], ps[:, c % 2, :], ACT.Copy).then_inc(xhi, 1)

                def split(g, o):
                    act.wait_ge(ro_ok, g + 1)
                    if not (isinstance(g, int) and g < 2):
                        act.wait_ge(stored[o % 2], 16 * (g - o % 2))
                    act.activation(pair[:, o % 2, 0, :], prod[:, o // 2 % 2, (EC, OC)[o % 2], :], ACT.Copy).then_inc(phi, 1)

                def evacuate(i, b, following, last=False):
                    n = 2 * i + b
                    for o in range(NT):
                        g = NT * n + o
                        act.wait_ge(proj, g + 1)
                        after(act, prod_ok, 3 * (NT // 2 * n + o // 2 - 1))
                        after(act, ec_ok, NT // 2 * n + o // 2 - 1)
                        act.activation(raw[:, o % 4, :], ps[:, 2 + o % 2, :], ACT.Copy, scale=1.0 / WS).then_inc(raw_ok, 1)
                        if o >= 2:
                            split(g - 2, o - 2)
                        if o == 6 and following:
                            root(*following)
                    for t in range(TB):
                        act.wait_ge(vps, TB * n + t + 1)
                        act.activation(v_all[:, b * H:(b + 1) * H, i * TB + t, :],
                                       ps[:, v_bank(t, last), :].rearrange("p (h d) -> p h d", h=H), ACT.Copy, scale=1.0 / WS).then_inc(v_ok, 1)
                        if t < 2:
                            split(NT * (n + 1) - 2 + t, NT - 2 + t)

                wt.high(act, 0)
                root(0, 0)
                high(0, 0)
                wt.high(act, 1)
                root(0, 1)
                high(0, 1)
                wt.high(act, 2)
                evacuate(0, 0, (1, 0))

                def two(i, last):
                    high(i, 0)
                    evacuate(i - 1, 1, (i, 1))
                    high(i, 1)
                    evacuate(i, 0, None if last else (i + 1, 0))

                with act.Fori(1, NBLK // 2 - 1) as i:
                    two(i, False)
                two(NBLK // 2 - 1, True)
                evacuate(NBLK // 2 - 1, 1, None, True)

            @block.gpsimd
            def _(pool):
                pool.memset(mxs.ks[MR:MR + 1, :, :], 1.0).then_inc(mxs.row_ok, 1)
                pool.wait_ge(mxs.row_ok, 1)
                pool.wait_ge(tab_in, 32)

                def body(i, b):
                    n = 2 * i + b
                    for o in range(0, NT, 2):
                        g, q = NT * n + o, NT // 2 * n + o // 2
                        even, odd = raw[:, o % 4, :], raw[:, o % 4 + 1, :]
                        apart(pool, pool_passed, (raw_ok, g + 1), (ro_ok, g - 2))
                        pool.tensor_tensor(prod[:, o // 2 % 2, ES, :], even, sin[:, bass.ds(i * BLK, BLK)], ALU.mult).then_inc(prod_ok, 1)
                        apart(pool, pool_passed, (raw_ok, g + 2), (phi, g - 2), (plo, g - 2))
                        pool.tensor_tensor(prod[:, o // 2 % 2, OS, :], odd, sin[:, bass.ds(i * BLK, BLK)], ALU.mult).then_inc(prod_ok, 1)
                        pool.tensor_tensor(prod[:, o // 2 % 2, OC, :], odd, cos[:, bass.ds(i * BLK, BLK)], ALU.mult).then_inc(prod_ok, 1)

                loop(pool, body)


def head_of(s):
    return (s // HS) % 2


def exists(it, s):
    return not (isinstance(it, int) and ITER * it + s >= NSTEP)


class Maxima:
    BANKS = (4, 5, 7)
    TURN_AT = 4

    def __init__(self, sb, sem, ps, ident, q_scr, k_scr, sum_ok, st):
        self.sum_ok = sum_ok
        self.ps, self.ident, self.q_scr, self.k_scr = ps, ident, q_scr, k_scr
        self.qs = sb("qs", [MR + 1, 2, S], F16, st)
        self.ks = sb("ks", [MR + 1, 2, S], F16, st)
        self.rmax = sb("rmax", [P, QT, KB], F32, st)
        self.m8 = sb("m8", [P, QT], F32, st)
        self.mrow = sb("mrow", [QT, P], F16, st)
        self.turn_bank = self.BANKS[self.TURN_AT % 3]
        self.row_ok = sem("row_ok", st)
        self.qk_in = [sem(f"qk_in{i}", st) for i in range(2)]
        self.mx = sem("mx", st)
        self.md = sem("md", st)
        self.m_all = sem("m_all", st)
        self.m_t = sem("m_t", st)
        self.m_r = sem("m_r", st)
        self.m_in = [sem(f"m_in{i}", st) for i in range(2)]

    def bank(self, i):
        return self.BANKS[(i + (i >= self.TURN_AT)) % 3]

    def load(self, sp, b, i, par):
        EH = DK // 2
        for scr, stack, halves in ((self.q_scr, self.qs, (0, 1, 0)), (self.k_scr, self.ks, (0, 0, 1))):
            for r, half in enumerate(halves):
                for e in range(2):
                    r0 = r * DK + e * EH
                    sp.dma_start(stack[r0:r0 + EH, par, :], scr[b, half, bass.ds(e * (D // 2) + (2 * i + par) * EH, EH), :])\
                        .then_inc(self.qk_in[par], 16)

    def store_max(self, sp, v):
        it, w = v
        u = 4 * it + w
        par, uh = w // UH, w % UH
        sp.wait_ge(self.m_r, u + 1)
        sp.dma_start(self.qs[MR:MR + 1, par, uh * UQ:(uh + 1) * UQ], self.mrow[:, :]).then_inc(self.m_in[par], 16)

    def scores(self, pe, it, s, j):
        if not exists(it, s):
            return
        par, uh, k = head_of(s), (s // KT) % UH, s % KT
        if s % HS == 0 and j == 0:
            pe.wait_ge(self.qk_in[par], 192 * (it + 1 + (0 if s < ITER else 1)))
        idx = 2 * k + j
        qt, kb = idx // KB, idx % KB
        u = UNITS * it + s // KT
        if idx == self.TURN_AT + 2:
            after(pe, self.m_r, u)
            if not (isinstance(u, int) and u < 3):
                pe.wait_ge(self.sum_ok, u - 2)
        if idx in (self.TURN_AT, self.TURN_AT + 1):
            after(pe, self.md, 2 * KT * u + idx - 1)
        else:
            after(pe, self.md, 2 * KT * u + idx - 2)
        q0 = uh * UQ + qt * P
        pe.matmul(self.ps[:, self.bank(idx), :], self.qs[0:SR, par, q0:q0 + P], self.ks[0:SR, par, kb * 512:(kb + 1) * 512],
                  start=True, stop=True).then_inc(self.mx, 1)

    def turn_max(self, pe, it, s, sums=None):
        if s % KT != self.TURN_AT // 2 - 1:
            return
        v = 4 * it + s // KT
        if isinstance(v, int) and (v == 0 or v > NU):
            return
        after(pe, self.md, 2 * KT * v + (self.TURN_AT - 2 if exists(it, s) else 0))
        if sums:
            sums()
        pe.wait_ge(self.m_all, v)
        pe.transpose(self.ps[0:QT, self.turn_bank, 0:P], self.m8[:, :], self.ident[:, :]).then_inc(self.m_t, 1)

    def reduce(self, dve, it, s, j):
        if not exists(it, s):
            return
        a = ITER * it + s
        u = 4 * it + s // KT
        idx = 2 * (s % KT) + j
        if idx == 0:
            after(dve, self.m_all, u)
        dve.wait_ge(self.mx, 2 * a + j + 1)
        dve.tensor_reduce(self.rmax[:, idx // KB, idx % KB:idx % KB + 1], self.ps[:, self.bank(idx), :], AX_X, ALU.max).then_inc(self.md, 1)
        if idx == 2 * KT - 1:
            dve.wait_ge(self.md, 2 * a + 2)
            after(dve, self.m_t, u)
            dve.tensor_reduce(self.m8[:, :], self.rmax[:, :, :], AX_X, ALU.max).then_inc(self.m_all, 1)

    def negate(self, dve, it, s):
        if s % KT != self.TURN_AT // 2 - 1:
            return
        v = 4 * it + s // KT
        if isinstance(v, int) and (v == 0 or v > NU):
            return
        dve.wait_ge(self.m_t, v)
        q = s // KT - 2
        if q >= 0:
            dve.wait_ge(self.m_in[q // UH], 16 * (UH * it + q % UH + 1))
        dve.tensor_scalar(self.mrow[:, :], self.ps[0:QT, self.turn_bank, 0:P], -1.0, None, ALU.mult).then_inc(self.m_r, 1)


class Normaliser:

    def __init__(self, sb, sem, r_scr, att_scr, st):
        self.r_scr, self.att_scr = r_scr, att_scr
        self.od = sb("od", [P, 2, 2 * QB], F32, st)
        self.d8 = sb("d8", [P, UQ // P], F32, st)
        self.r8 = sb("r8", [P, UQ // P], F32, st)
        self.rb = sb("rb", [P, QB], F32, st)
        self.on = sb("on", [P, QB], F32, st)
        self.od_ok = sem("od_ok", st)
        self.sum_ok = sem("sum_ok", st)
        self.d8_in = sem("d8_in", st)
        self.r8_ok = sem("r8_ok", st)
        self.r8_out = sem("r8_out", st)
        self.rb_in = sem("rb_in", st)
        self.on_ok = sem("on_ok", st)
        self.at_out = sem("at_out", st)

    def invert(self, sp, b, i, w):
        u, p = UNITS * (H // 2 * b + i) + w, w % 2
        if isinstance(u, int) and u == NU - 1:
            sp.wait_ge(self.od_ok, u + 1)
        else:
            sp.wait_ge(self.sum_ok, u + 1)
        sp.dma_start(self.d8[:, :], self.od[0:P:DK, p, QB:2 * QB]).then_inc(self.d8_in, 16)
        sp.wait_ge(self.r8_ok, u + 1)
        sp.dma_start(self.r_scr[p].rearrange("(p e) -> p e", p=P), self.r8[:, :]).then_inc(self.r8_out, 16)
        sp.wait_ge(self.r8_out, 16 * (u + 1))
        for j in range(4):
            sp.dma_start(self.rb[j * DK:(j + 1) * DK, :],
                         self.r_scr[p:p + 1, j * QB:(j + 1) * QB].broadcast_to([DK, QB])).then_inc(self.rb_in, 16)

    def store(self, sp, b, i, w):
        u = UNITS * (H // 2 * b + i) + w
        par, uh = w // UH, w % UH
        sp.wait_ge(self.on_ok, u + 1)
        for j in range(4):
            q0 = uh * UQ + j * QB
            sp.dma_start(self.att_scr[bass.ds((2 * i + par) * DK, DK), b * S + q0:b * S + q0 + QB],
                         self.on[j * DK:(j + 1) * DK, :]).then_inc(self.at_out, 16)

    def reciprocal(self, dve, it, w):
        u = UNITS * it + w + 1
        dve.wait_ge(self.d8_in, 16 * u)
        after(dve, self.r8_out, 16 * (u - 1))
        dve.reciprocal(self.r8[:, :], self.d8[:, :]).then_inc(self.r8_ok, 1)

    def multiply(self, dve, it, w):
        u = UNITS * it + w + 1
        dve.wait_ge(self.rb_in, 64 * u)
        after(dve, self.at_out, 64 * (u - 1))
        dve.tensor_tensor(self.on[:, :], self.od[:, w % 2, 0:QB], self.rb[:, :], ALU.mult).then_inc(self.on_ok, 1)


def attend(nc, sb, sem, ps, v_all, mxs, nrm, late, prefetch):
    NPA = len(POOL_TILES) - 1
    SUM_AT = (mxs.TURN_AT // 2 - 1 - AHEAD) % KT
    NHEAD = B * H
    qs, ks = mxs.qs, mxs.ks
    with ExitStack() as st:
        late.buffers(st)
        vh = sb("vh", [P, 2, KT, DK], F32, st)
        ones = sb("ones", [P, DK], F32, st)
        psum_p = sb("psum_p", [P, 2, UQ], F32, st)
        pr = sb("pr", [P, NP, UQ], F32, st)
        init = sem("init", st)
        v_copied = sem("v_copied", st)
        sc = sem("sc", st)
        ex = sem("ex", st)
        pv = sem("pv", st)
        ps_p = sem("ps_p", st)
        rs_p = sem("rs_p", st)
        passed = sem("passed", st)

        SC, OV = 0, 6
        def late_job(it, s):
            r = s - (ITER - AHEAD)
            if not isinstance(it, int) or it != NHEAD // 2 - 1 or r < 0:
                return None, False
            j = (r - 3) // 2
            return (j if r >= 3 and r % 2 and j < len(late.jobs) else None), r == 0

        def sweep(eng, step):
            for s in range(ITER):
                step(0, s)
            with eng.Fori(1, NHEAD // 2 - 1) as it:
                for s in range(ITER):
                    step(it, s)
            for s in range(ITER):
                step(NHEAD // 2 - 1, s)

        def adds(tiles, it, s):
            upto = sum(1 for k in tiles if k <= s % KT)
            return (len(tiles) - 1) * (UNITS * it + s // KT) + (max(1, upto - 1) if upto else 0)

        with nc.Block() as block:
            @block.gpsimd
            def _(pool):
                pool.memset(ones[:, :], 1.0).then_inc(init, 1)
                pool.wait_ge(init, 1)

                def step(it, s):
                    k, u = s % KT, UNITS * it + s // KT
                    if k in POOL_TILES[1:]:
                        n = POOL_TILES.index(k)
                        pool.wait_ge(ex, ITER * it + s + 1)
                        acc = psum_p[:, (s // KT) % 2, :]
                        if n == 1:
                            after(pool, rs_p, u - 1)
                            first = pr[:, (s - k + POOL_TILES[0]) % NP, :]
                        else:
                            after(pool, ps_p, NPA * u + n - 1)
                            first = acc
                        pool.tensor_tensor(acc, first, pr[:, s % NP, :], ALU.add).then_inc(ps_p, 1)

                sweep(pool, step)

            @block.sync
            def _(sp):
                late.load(sp)

                def heads(b, i, before, last):
                    base = H // 2 * b + i
                    nb, ni = (b + 1, 0) if isinstance(i, int) and i + 1 == H // 2 else (b, i + 1)
                    if before:
                        nrm.store(sp, *before, UNITS - 2)
                    mxs.store_max(sp, (base, 1))
                    if before:
                        nrm.invert(sp, *before, UNITS - 1)
                        nrm.store(sp, *before, UNITS - 1)
                    mxs.store_max(sp, (base, 2))
                    nrm.invert(sp, b, i, 0)
                    if not last:
                        sp.wait_ge(sc, ITER * base + HS)
                        mxs.load(sp, nb, ni, 0)
                    nrm.store(sp, b, i, 0)
                    mxs.store_max(sp, (base, 3))
                    nrm.invert(sp, b, i, 1)
                    nrm.store(sp, b, i, 1)
                    if last:
                        sp.wait_ge(nrm.at_out, 64 * NU // B)
                        prefetch(sp)
                    else:
                        mxs.store_max(sp, (base + 1, 0))
                    nrm.invert(sp, b, i, 2)
                    if last:
                        nrm.store(sp, b, i, 2)
                    else:
                        sp.wait_ge(sc, ITER * base + 2 * HS)
                        mxs.load(sp, nb, ni, 1)

                for b in range(B):
                    heads(b, 0, (b - 1, H // 2 - 1) if b else None, False)
                    with sp.Fori(1, H // 2 - 1) as i:
                        heads(b, i, (b, i - 1), False)
                    heads(b, H // 2 - 1, (b, H // 2 - 2), b == B - 1)

            @block.tensor
            def _(pe):
                pe.wait_ge(init, 1)
                pe.wait_ge(mxs.row_ok, 1)

                def scores(it, s):
                    g = ITER * it + s
                    par, uh, k = head_of(s), (s // KT) % UH, s % KT
                    if k == 0:
                        pe.wait_ge(mxs.m_in[par], 16 * (UH * it + uh + 1))
                    after(pe, ex, g - 1)
                    for j in range(2):
                        q0 = uh * UQ + j * 512
                        ins = pe.matmul(ps[:, SC + 2 * (s % 2) + j, :], ks[:, par, k * P:(k + 1) * P], qs[:, par, q0:q0 + 512],
                                        start=True, stop=True)
                    ins.then_inc(sc, 1)

                def values(it, s):
                    g = ITER * it + s
                    par, k = head_of(s), s % KT
                    if s % HS == 0:
                        pe.wait_ge(v_copied, 2 * it + par + 1)
                    if k == 0:
                        after(pe, nrm.od_ok, UNITS * it + s // KT)
                    pe.wait_ge(ex, g + 1)
                    for j in range(4):
                        ins = pe.matmul(ps[DK * j:DK * j + DK, OV, 0:QB], vh[:, par, k, :], pr[:, s % NP, j * QB:(j + 1) * QB],
                                        start=(k == 0), stop=(k == KT - 1), skip_group_check=True,
                                        tile_position=(0, DK * j))
                    if k not in POOL_TILES:
                        ins = row_sums(pr[:, s % NP, :])
                    ins.then_inc(pv, 1)
                    if isinstance(it, int) and g == NSTEP - 1:
                        pe.wait_ge(ps_p, NPA * NU)
                        row_sums(psum_p[:, (s // KT) % 2, :]).then_inc(rs_p, 1)

                def row_sums(p, bank=OV, start=False):
                    for j in range(4):
                        ins = pe.matmul(ps[DK * j:DK * j + DK, bank, QB:2 * QB], ones[:, :], p[:, j * QB:(j + 1) * QB],
                                        start=start, stop=False, skip_group_check=True, tile_position=(0, DK * j))
                    return ins

                def step(it, s):
                    scores(it, s)
                    sa = s + AHEAD
                    mxs.scores(pe, it, sa, 0)
                    if s >= 1:
                        values(it, s - 1)
                    elif not (isinstance(it, int) and it == 0):
                        values(it - 1, ITER - 1)
                    mxs.scores(pe, it, sa, 1)

                    def sums():
                        pe.wait_ge(ps_p, NPA * (UNITS * it + s // KT))
                        row_sums(psum_p[:, (s // KT - 1) % 2, :], mxs.turn_bank, True).then_inc(rs_p, 1)

                    if isinstance(it, int) and UNITS * it + s // KT == NU - 1:
                        if s % KT == SUM_AT:
                            pe.wait_ge(nrm.sum_ok, NU - 2)
                            sums()
                    else:
                        mxs.turn_max(pe, it, sa, None if isinstance(it, int) and it == 0 and s < KT else sums)
                    j, _ = late_job(it, s)
                    if j is not None:
                        if j == 0:
                            pe.wait_ge(mxs.md, 2 * NSTEP)
                            pe.wait_ge(mxs.m_r, NU)
                        late.turn(pe, j)

                sweep(pe, step)
                values(NHEAD // 2 - 1, ITER - 1)

            @block.scalar
            def _(act):
                def evacuate(u, p):
                    act.wait_ge(pv, KT * u)
                    if isinstance(u, int) and u == NU:
                        act.wait_ge(rs_p, NU)
                    after(act, nrm.on_ok, u - 2)
                    act.activation(nrm.od[:, p, :], ps[:, OV, :], ACT.Copy).then_inc(nrm.od_ok, 1)

                def copy(it, par):
                    apart(act, passed, (pv, HS * (2 * it + par - 1)))
                    act.activation(vh[:, par, :, :], v_all[:, 2 * it + par, :, :], ACT.Copy).then_inc(v_copied, 1)

                def step(it, s):
                    g = ITER * it + s
                    act.wait_ge(sc, g + 1)
                    after(act, pv, g - NP + 1)
                    if (s - NP) % KT in POOL_TILES:
                        after(act, ps_p, adds(POOL_TILES, it, s - NP))
                    act.activation(pr[:, s % NP, :], ps[:, SC + 2 * (s % 2):SC + 2 * (s % 2) + 2, :].rearrange("p a n -> p (a n)"),
                                   ACT.Exp, scale=SM_SCALE).then_inc(ex, 1)
                    if s % KT == 0 and not (isinstance(it, int) and g == 0):
                        evacuate(UNITS * it + s // KT, (s // KT - 1) % 2)
                    if s % HS == 11:
                        if s < HS:
                            copy(it, 1)
                        elif not (isinstance(it, int) and it == NHEAD // 2 - 1):
                            copy(it + 1, 0)
                    j, start = late_job(it, s)
                    if start:
                        late.ctx_high(act)
                    if j is not None:
                        late.high(act, j)

                copy(0, 0)
                sweep(act, step)
                evacuate(NU, 1)

            @block.vector
            def _(dve):
                def add_sums(dve, it, w):
                    u = UNITS * it + w + 1
                    dve.wait_ge(nrm.od_ok, u)
                    dve.wait_ge(rs_p, u)
                    sums = nrm.od[:, w % 2, QB:2 * QB]
                    dve.tensor_tensor(sums, ps[:, mxs.turn_bank, QB:2 * QB], sums, ALU.add).then_inc(nrm.sum_ok, 1)

                def step(it, s):
                    for j in range(2):
                        mxs.reduce(dve, it, s + AHEAD, j)
                    mxs.negate(dve, it, s + AHEAD)
                    j, start = late_job(it, s)
                    if start:
                        late.early(dve)
                    if j is not None:
                        late.low(dve, j)
                    for at, do, back in ((SUM_AT, add_sums, 1), (13, nrm.reciprocal, 1), (4, nrm.multiply, 2)):
                        if s % KT == at:
                            w = s // KT - back
                            if w >= 0:
                                do(dve, it, w)
                            elif not (isinstance(it, int) and it == 0):
                                do(dve, it - 1, w + UNITS)

                sweep(dve, step)
                nrm.multiply(dve, NHEAD // 2 - 1, UNITS - 2)


class TailInputs:

    def __init__(self, sb, sem, x_s, att_scr, st):
        TT = TBLK // P
        self.x_s, self.att = x_s, att_scr.rearrange("(c p) (b s) -> b p c s", p=P, b=B)
        self.xin = sb("xin3", [P, 2, TT, D], F32, st)
        self.aT = sb("aT", [P, 2, CH, TBLK], F32, st)
        self.x_in = [sem(f"x_in3{p}", st) for p in range(2)]
        self.a_in = [sem(f"a_in3{p}", st) for p in range(2)]

    def load_attention(self, sp, b, i, par):
        sp.dma_start(self.aT[:, par, :, :], self.att[b][:, :, bass.ds(i * TBLK, TBLK)]).then_inc(self.a_in[par], 16)

    def load_x(self, sp, b, i, par):
        sp.dma_start(self.xin[:, par, :, :], self.x_s[b, i]).then_inc(self.x_in[par], 16)

    def first(self, sp):
        for i in range(2):
            self.load_attention(sp, 0, i, i)
            self.load_x(sp, 0, i, i)


def tail(nc, sb, sem, ps, wT, wfT, ctxT, ctxr, ident, fsc, fbi, inputs, nrm, out_s):
    TT = TBLK // P
    NB = NTOK // TBLK
    G = 4
    HC = CH // 2
    with ExitStack() as st:
        xin, aT, x_in, a_in = inputs.xin, inputs.aT, inputs.x_in, inputs.a_in
        xr = sb("xr", [P, G, TT, D], F32, st)
        aP = sb("aP", [P, 2, 2, CH, TBLK], F16, st)
        xh1 = sb("xh1", [P, TT, D], F32, st)
        xh2 = sb("xh2", [P, TT, D], F32, st)
        xT1 = sb("xT1", [P, 2, CH, TBLK], F16, st)
        xT2 = sb("xT2", [P, 2, CH, TBLK], F16, st)
        gf = sb("gf", [T, TBLK], F32, st)
        gT = sb("gT", [T, 2, TBLK], F16, st)
        y = sb("y", [P, 2, TT, D], F32, st)
        stat = sb("stat3", [P, 2, TT, 6], F32, st)
        mv = sb("mv3", [P, 2, TT, 2], F32, st)
        var = sb("var3", [P, 2, TT], F32, st)
        std = sb("std3", [P, 2, TT], F32, st)
        rstd = sb("rstd3", [P, 2, TT], F32, st)
        o_out = [sem(f"o_out{p}", st) for p in range(2)]
        a_hi, a_lo = sem("a_hi", st), sem("a_lo", st)
        turned = {g: sem(f"turned_{g}", st) for g in "BD"}
        t_hi = {g: sem(f"t_hi_{g}", st) for g in "BD"}
        t_lo = {g: sem(f"t_lo_{g}", st) for g in "BD"}
        tile = {g: sem(f"tile_{g}", st) for g in "ACD"}
        taken = {g: sem(f"taken_{g}", st) for g in "ACD"}
        h_ok, g_ok, g_hi, g_lo = sem("h_ok", st), sem("g_ok", st), sem("g_hi", st), sem("g_lo", st)
        stats = [sem(f"stats3{k}", st) for k in range(2)]
        aggr = [sem(f"aggr3{k}", st) for k in range(2)]
        var_ok = [sem(f"var_ok3{k}", st) for k in range(2)]
        std_ok = [sem(f"std_ok3{k}", st) for k in range(2)]
        rstd_ok = [sem(f"rstd_ok3{k}", st) for k in range(2)]
        normed = [sem(f"normed3{k}", st) for k in range(2)]
        biased, clipped, final = sem("biased", st), sem("clipped", st), sem("final", st)
        last_biased, last_clipped, last_final = sem("last_biased", st), sem("last_clipped", st), sem("last_final", st)
        dve_passed, pool_passed, sp_passed = sem("dve_passed3", st), sem("pool_passed3", st), sem("sp_passed3", st)
        A_BANK, C_BANK, D_BANK, H_BANK = 6, 4, 4, 0
        T_BANK = {"D": 0, "B": 2}
        SPLITS = ((0, 0), (1, 0), (0, 1))

        class Slot:

            def __init__(self, k, r):
                self.k, self.r = k, r

            def block(self, off):
                k, r = self.k, self.r - off
                m = G * k + r
                if isinstance(m, int) and not 0 <= m < NB:
                    return None
                return m, r % G // 2, 2 * k + (2 * (r // G) + r % 2), r % G, r % 2, 2 * k + r // 2

        def slots(eng, body):
            for r in range(G):
                body(Slot(0, r))
            with eng.Fori(1, NB // G - 1) as k:
                for r in range(G):
                    body(Slot(k, r))
            for r in range(G + 3):
                body(Slot(NB // G - 1, r))

        with nc.Block() as block:
            @block.sync
            def _(sp):
                def load_attention(sl, off):
                    if blk := sl.block(off):
                        m, b, i, _, par, _ = blk
                        after(sp, a_hi, m - 1)
                        after(sp, a_lo, m - 1)
                        inputs.load_attention(sp, b, i, par)

                def load_x(sl, off):
                    if blk := sl.block(off):
                        m, b, i, _, par, _ = blk
                        after(sp, taken["A"], TT * (m - 1))
                        inputs.load_x(sp, b, i, par)

                def store(sl):
                    if blk := sl.block(3):
                        m, b, i, _, par, _ = blk
                        if isinstance(m, int) and m == NB - 1:
                            sp.wait_ge(last_final, TT)
                        else:
                            apart(sp, sp_passed, (final, TT * (m + 1)))
                        sp.dma_start(out_s[b, i], y[:, par, :, :]).then_inc(o_out[par], 16)

                def body(sl):
                    load_attention(sl, -2)
                    load_x(sl, -2)
                    store(sl)

                nrm.invert(sp, B - 1, H // 2 - 1, UNITS - 1)
                nrm.store(sp, B - 1, H // 2 - 1, UNITS - 1)
                sp.wait_ge(nrm.at_out, 64 * NU)
                slots(sp, body)
                for b in range(2):
                    sp.wait_ge(o_out[b], 16 * NB // 2)

            @block.tensor
            def _(pe):
                def turn(g, sl, off, src, k):
                    if not (blk := sl.block(off)):
                        return
                    m = blk[0]
                    pe.wait_ge(normed[k], TT * (m + 1))
                    if g == "D":
                        pe.wait_ge(g_ok, min(m + 2, NB) if isinstance(m, int) else m + 2)
                    after(pe, t_lo[g], HC * m)
                    for c in range(CH):
                        for t in range(TT):
                            o = (c % 2) * TBLK + t * P
                            ins = pe.transpose(ps[:, T_BANK[g] + c // 2, o:o + P], src[:, t, c * P:(c + 1) * P], ident[:, :])
                        if c % 2:
                            ins.then_inc(turned[g], 1)

                def tiles(g, bank, m, terms):
                    for t in range(TT):
                        pairs = terms(t)
                        for k, (lhs, rhs) in enumerate(pairs):
                            ins = pe.matmul(ps[:, bank + t, :], lhs, rhs, start=(k == 0), stop=(k == len(pairs) - 1))
                        ins.then_inc(tile[g], 1)

                def body(sl):
                    turn("D", sl, 3, xh2, 1)
                    turn("B", sl, 1, xh1, 0)
                    if blk := sl.block(2):
                        m, b = blk[:2]
                        pe.wait_ge(g_lo, m + 1)
                        after(pe, taken["D"], TT * (m - 1))
                        tiles("C", C_BANK, m, lambda t: [(gT[:, a, t * P:(t + 1) * P], ctxr[:, b, r, :]) for a, r in SPLITS])
                    if blk := sl.block(0):
                        m, par = blk[0], blk[4]
                        pe.wait_ge(a_lo, m + 1)
                        after(pe, taken["A"], TT * m)
                        tiles("A", A_BANK, m, lambda t: [(aP[:, par, a, c, t * P:(t + 1) * P], wT["wo"][:, r, c, :])
                                                         for c in range(CH) for a, r in SPLITS])
                    if blk := sl.block(3):
                        m = blk[0]
                        pe.wait_ge(t_lo["D"], HC * (m + 1))
                        pe.wait_ge(taken["C"], TT * min(m + 2, NB) if isinstance(m, int) else TT * (m + 2))
                        tiles("D", D_BANK, m, lambda t: [(xT2[:, a, c, t * P:(t + 1) * P], wfT[:, c, :])
                                                         for c in range(CH) for a in (0, 1)])
                    if blk := sl.block(1):
                        m, b = blk[:2]
                        pe.wait_ge(t_lo["B"], HC * (m + 1))
                        after(pe, t_lo["D"], HC * (m - 1))
                        after(pe, g_ok, m)
                        n = 0
                        for c in range(CH):
                            for a, r in SPLITS:
                                ins = pe.matmul(ps[0:T, H_BANK, 0:TBLK], ctxT[:, b, a, c, :], xT1[:, r, c, :],
                                                start=(n == 0), stop=(n == 3 * CH - 1))
                                n += 1
                        ins.then_inc(h_ok, 1)

                slots(pe, body)

            @block.scalar
            def _(act):
                def attention(sl, off):
                    if not (blk := sl.block(off)):
                        return
                    m, par, count = blk[0], blk[4], blk[5]
                    act.wait_ge(a_in[par], 16 * (count + 1))
                    after(act, tile["A"], TT * (m - 1))
                    act.activation(aP[:, par, 0, :, :], aT[:, par, :, :], ACT.Copy).then_inc(a_hi, 1)

                def high(g, sl, off, dst):
                    if not (blk := sl.block(off)):
                        return
                    for c in range(HC):
                        act.wait_ge(turned[g], HC * blk[0] + c + 1)
                        act.activation(dst[:, 0, 2 * c:2 * c + 2, :], ps[:, T_BANK[g] + c, :].rearrange("p (a t) -> p a t", a=2),
                                       ACT.Copy).then_inc(t_hi[g], 1)

                def root(k, sl, off):
                    if not (blk := sl.block(off)):
                        return
                    act.wait_ge(var_ok[k], blk[0] + 1)
                    act.activation(std[:, k, :], var[:, k, :], ACT.Sqrt).then_inc(std_ok[k], 1)

                def body(sl):
                    high("D", sl, 3, xT2)
                    high("B", sl, 1, xT1)
                    root(1, sl, 2)
                    attention(sl, -1)
                    root(0, sl, 0)
                    if blk := sl.block(1):
                        m = blk[0]
                        act.wait_ge(h_ok, m + 1)
                        after(act, g_lo, m)
                        act.activation(gf[:, :], ps[0:T, H_BANK, 0:TBLK], ACT.Gelu_apprx_tanh, scale=1.0 / WS).then_inc(g_ok, 1)
                        act.wait_ge(g_ok, m + 1)
                        act.activation(gT[:, 0, :], gf[:, :], ACT.Copy).then_inc(g_hi, 1)

                attention(Slot(0, 0), 0)
                slots(act, body)

            @block.vector
            def _(dve):
                def low(g, sl, off, dst):
                    if not (blk := sl.block(off)):
                        return
                    for c in range(HC):
                        dve.wait_ge(t_hi[g], HC * blk[0] + c + 1)
                        dve.tensor_tensor(dst[:, 1, 2 * c:2 * c + 2, :], ps[:, T_BANK[g] + c, :].rearrange("p (a t) -> p a t", a=2),
                                          dst[:, 0, 2 * c:2 * c + 2, :], ALU.subtract).then_inc(t_lo[g], 1)

                def norm(k, g, m, ring, dst, turned_g):
                    dve.wait_ge(taken[g], TT * (m + 1))
                    for t in range(TT):
                        dve.bn_stats(stat[:, k, t, :], xr[:, ring, t, :]).then_inc(stats[k], 1)
                    apart(dve, dve_passed, (stats[k], TT * (m + 1)), (normed[k], TT * m))
                    for t in range(TT):
                        dve.bn_aggr(mv[:, k, t, :], stat[:, k, t, :]).then_inc(aggr[k], 1)
                    dve.wait_ge(aggr[k], TT * (m + 1))
                    dve.tensor_scalar(var[:, k, :], mv[:, k, :, 1], EPS, None, ALU.add).then_inc(var_ok[k], 1)
                    dve.wait_ge(std_ok[k], m + 1)
                    dve.reciprocal(rstd[:, k, :], std[:, k, :]).then_inc(rstd_ok[k], 1)
                    dve.wait_ge(rstd_ok[k], m + 1)
                    after(dve, turned[turned_g], HC * m)
                    for t in range(TT):
                        dve.tensor_scalar(dst[:, t, :], xr[:, ring, t, :], mv[:, k, t, 0:1], rstd[:, k, t:t + 1],
                                          ALU.subtract, ALU.mult).then_inc(normed[k], 1)

                def body(sl):
                    low("D", sl, 3, xT2)
                    low("B", sl, 1, xT1)
                    if blk := sl.block(2):
                        m, ring = blk[0], blk[3]
                        for t in range(TT):
                            dve.wait_ge(tile["C"], TT * m + t + 1)
                            dve.scalar_tensor_tensor(xr[:, ring, t, :], ps[:, C_BANK + t, :], 1.0 / WS, xr[:, ring, t, :],
                                                     ALU.mult, ALU.add).then_inc(taken["C"], 1)
                        norm(1, "C", m, ring, xh2, "D")
                    if blk := sl.block(0):
                        m, _, _, ring, par, count = blk
                        dve.wait_ge(x_in[par], 16 * (count + 1))
                        after(dve, final, TT * (m - G + 1))
                        for t in range(TT):
                            dve.wait_ge(tile["A"], TT * m + t + 1)
                            dve.scalar_tensor_tensor(xr[:, ring, t, :], ps[:, A_BANK + t, :], 1.0 / WS, xin[:, par, t, :],
                                                     ALU.mult, ALU.add).then_inc(taken["A"], 1)
                        norm(0, "A", m, ring, xh1, "B")
                    if blk := sl.block(3):
                        m, par, count = blk[0], blk[4], blk[5]
                        after(dve, o_out[par], 16 * count)
                        for t in range(TT):
                            dve.wait_ge(tile["D"], TT * m + t + 1)
                            dve.tensor_tensor(y[:, par, t, :], ps[:, D_BANK + t, :], fsc[:, :], ALU.mult).then_inc(taken["D"], 1)
                        if isinstance(m, int) and m == NB - 1:
                            finish(blk)
                    if blk := sl.block(1):
                        dve.wait_ge(g_hi, blk[0] + 1)
                        dve.tensor_tensor(gT[:, 1, :], gf[:, :], gT[:, 0, :], ALU.subtract).then_inc(g_lo, 1)

                def finish(blk):
                    m, ring, par = blk[0], blk[3], blk[4]
                    for t in range(TT):
                        dve.wait_ge(taken["D"], TT * m + t + 1)
                        dve.tensor_tensor(y[:, par, t, :], y[:, par, t, :], fbi[:, :], ALU.add).then_inc(last_biased, 1)
                    for t in range(TT):
                        dve.wait_ge(last_biased, t + 1)
                        dve.tensor_scalar(y[:, par, t, :], y[:, par, t, :], CLIP, -CLIP, ALU.min, ALU.max).then_inc(last_clipped, 1)
                    for t in range(TT):
                        dve.wait_ge(last_clipped, t + 1)
                        dve.tensor_tensor(y[:, par, t, :], y[:, par, t, :], xr[:, ring, t, :], ALU.add).then_inc(last_final, 1)

                def first_body(sl):
                    body(sl)
                    if isinstance(sl.k, int) and (sl.k, sl.r) == (0, 0):
                        nrm.multiply(dve, NU // UNITS - 1, UNITS - 1)

                nrm.reciprocal(dve, NU // UNITS - 1, UNITS - 1)
                slots(dve, first_body)

            @block.gpsimd
            def _(pool):
                def attention(sl, off):
                    if not (blk := sl.block(off)):
                        return
                    m, par = blk[0], blk[4]
                    pool.wait_ge(a_hi, m + 1)
                    pool.tensor_tensor(aP[:, par, 1, :, :], aT[:, par, :, :], aP[:, par, 0, :, :], ALU.subtract).then_inc(a_lo, 1)

                def body(sl):
                    attention(sl, -1)
                    if blk := sl.block(3):
                        m, _, _, ring, par, _ = blk
                        if isinstance(m, int) and m == NB - 1:
                            return
                        for t in range(TT):
                            n = TT * m + t
                            pool.wait_ge(taken["D"], n + 1)
                            pool.tensor_tensor(y[:, par, t, :], y[:, par, t, :], fbi[:, :], ALU.add).then_inc(biased, 1)
                            apart(pool, pool_passed, (biased, n + 1))
                            pool.tensor_scalar(y[:, par, t, :], y[:, par, t, :], CLIP, -CLIP, ALU.min, ALU.max).then_inc(clipped, 1)
                            pool.wait_ge(clipped, n + 1)
                            pool.tensor_tensor(y[:, par, t, :], y[:, par, t, :], xr[:, ring, t, :], ALU.add).then_inc(final, 1)

                attention(Slot(0, 0), 0)
                slots(pool, body)

_INS = ["x", "ctx_1024", "L0_attn_W_q", "L0_attn_W_k", "L0_attn_W_v", "L0_attn_W_o",
        "L0_ffn_weights", "L0_ffn_scale", "L0_ffn_bias"]


def _constants():
    f = np.float32
    ident = np.eye(P, dtype=f)
    inv_freq = f(1.0) / np.power(f(10000.0), np.arange(0, DK, 2, dtype=f) / f(DK)).astype(f)
    angle = (np.arange(S, dtype=f)[None, :] * inv_freq[np.arange(P) % (DK // 2)][:, None]).astype(f)
    return {"ident": ident, "cos": np.cos(angle).astype(f), "sin": np.sin(angle).astype(f)}


def kernel(**inputs):
    import concourse.bacc as _bacc
    from concourse.bass_utils import run_bass_kernel_spmd as _run

    nc = _bacc.Bacc("TRN2", target_bir_lowering=False, num_devices=1)
    arrays, args = {}, []
    for name in _INS:
        a = np.ascontiguousarray(inputs[name])
        arrays[f"in_{name}"] = a
        args.append(nc.dram_tensor(f"in_{name}", a.shape, mybir.dt.from_np(a.dtype), kind="ExternalInput").ap())
    for name, a in _constants().items():
        arrays[f"const_{name}"] = a
        args.append(nc.dram_tensor(f"const_{name}", a.shape, mybir.dt.from_np(a.dtype), kind="ExternalInput").ap())
    args.append(nc.dram_tensor("out_0", (B, S, D), F32, kind="ExternalOutput").ap())
    decoder_layer(nc, *args)
    r = _run(nc, [arrays], core_ids=[0])
    return r.results[0]["out_0"]
```
